# Optimizing a Trainium2 kernel written in Bass

```python
import numpy as np
import jax
import jax.numpy as jnp

def _softmax(x, axis=-1):
    return jax.nn.softmax(x, axis=axis)

def _gelu(x):
    return jax.nn.gelu(x, approximate=True)

def _silu(x):
    return jax.nn.silu(x)

def _sigmoid(x):
    return jax.nn.sigmoid(x)

def _layernorm(x, axis=-1, eps=1e-05):
    m = jnp.mean(x, axis=axis, keepdims=True)
    v = jnp.var(x, axis=axis, keepdims=True)
    return (x - m) / jnp.sqrt(v + eps)

def _scatter_add(tgt, idx, src, axis=0):
    return tgt.at[idx].add(src)

def _segment_sum(src, seg, n):
    return jax.ops.segment_sum(src, seg, n)
kernel_name = 'mk_dlrm_tower_d1_rec_r8_6693c5'

def setup_inputs(seed: int=0):
    np.random.seed(seed)
    _w = jnp.asarray

    def _rec_inputs():
        import jax
        import jax.numpy as jnp
        _tk = jax.random.key(seed)
        ids = jnp.stack([jax.random.randint(jax.random.fold_in(_tk, 200 + f), (512,), 0, v, jnp.int32) for f, v in enumerate([12500, 1000, 12500, 1000, 1000, 1000, 12500, 125000, 1250, 125000, 125000, 1250, 12500, 1250, 12500, 1000, 1250, 1250, 1250, 12500, 1250, 1250, 1250, 12500, 12500, 1250])], axis=1)
        tbl_0 = 0.05 * jax.random.normal(jax.random.fold_in(_tk, 500 + 0), (12500, 64), jnp.float32)
        tbl_1 = 0.05 * jax.random.normal(jax.random.fold_in(_tk, 500 + 1), (1000, 64), jnp.float32)
        tbl_2 = 0.05 * jax.random.normal(jax.random.fold_in(_tk, 500 + 2), (12500, 64), jnp.float32)
        tbl_3 = 0.05 * jax.random.normal(jax.random.fold_in(_tk, 500 + 3), (1000, 64), jnp.float32)
        tbl_4 = 0.05 * jax.random.normal(jax.random.fold_in(_tk, 500 + 4), (1000, 64), jnp.float32)
        tbl_5 = 0.05 * jax.random.normal(jax.random.fold_in(_tk, 500 + 5), (1000, 64), jnp.float32)
        tbl_6 = 0.05 * jax.random.normal(jax.random.fold_in(_tk, 500 + 6), (12500, 64), jnp.float32)
        tbl_7 = 0.05 * jax.random.normal(jax.random.fold_in(_tk, 500 + 7), (125000, 64), jnp.float32)
        tbl_8 = 0.05 * jax.random.normal(jax.random.fold_in(_tk, 500 + 8), (1250, 64), jnp.float32)
        tbl_9 = 0.05 * jax.random.normal(jax.random.fold_in(_tk, 500 + 9), (125000, 64), jnp.float32)
        tbl_10 = 0.05 * jax.random.normal(jax.random.fold_in(_tk, 500 + 10), (125000, 64), jnp.float32)
        tbl_11 = 0.05 * jax.random.normal(jax.random.fold_in(_tk, 500 + 11), (1250, 64), jnp.float32)
        tbl_12 = 0.05 * jax.random.normal(jax.random.fold_in(_tk, 500 + 12), (12500, 64), jnp.float32)
        tbl_13 = 0.05 * jax.random.normal(jax.random.fold_in(_tk, 500 + 13), (1250, 64), jnp.float32)
        tbl_14 = 0.05 * jax.random.normal(jax.random.fold_in(_tk, 500 + 14), (12500, 64), jnp.float32)
        tbl_15 = 0.05 * jax.random.normal(jax.random.fold_in(_tk, 500 + 15), (1000, 64), jnp.float32)
        tbl_16 = 0.05 * jax.random.normal(jax.random.fold_in(_tk, 500 + 16), (1250, 64), jnp.float32)
        tbl_17 = 0.05 * jax.random.normal(jax.random.fold_in(_tk, 500 + 17), (1250, 64), jnp.float32)
        tbl_18 = 0.05 * jax.random.normal(jax.random.fold_in(_tk, 500 + 18), (1250, 64), jnp.float32)
        tbl_19 = 0.05 * jax.random.normal(jax.random.fold_in(_tk, 500 + 19), (12500, 64), jnp.float32)
        tbl_20 = 0.05 * jax.random.normal(jax.random.fold_in(_tk, 500 + 20), (1250, 64), jnp.float32)
        tbl_21 = 0.05 * jax.random.normal(jax.random.fold_in(_tk, 500 + 21), (1250, 64), jnp.float32)
        tbl_22 = 0.05 * jax.random.normal(jax.random.fold_in(_tk, 500 + 22), (1250, 64), jnp.float32)
        tbl_23 = 0.05 * jax.random.normal(jax.random.fold_in(_tk, 500 + 23), (12500, 64), jnp.float32)
        tbl_24 = 0.05 * jax.random.normal(jax.random.fold_in(_tk, 500 + 24), (12500, 64), jnp.float32)
        tbl_25 = 0.05 * jax.random.normal(jax.random.fold_in(_tk, 500 + 25), (1250, 64), jnp.float32)
        _rk = jax.random.fold_in(_tk, 7)
        r_dense_t = 7.22013e-05 + 1.00017 * jax.random.normal(jax.random.fold_in(_rk, 101), (512, 256), jnp.float32)
        W_top1 = 0.0360844 * jax.random.normal(jax.random.fold_in(_tk, 801), (768, 512), jnp.float32)
        W_top2 = 0.0441942 * jax.random.normal(jax.random.fold_in(_tk, 802), (512, 256), jnp.float32)
        W_top3 = 0.0625 * jax.random.normal(jax.random.fold_in(_tk, 803), (256, 1), jnp.float32)
        b_top1 = jnp.zeros((512,), jnp.float32)
        b_top2 = jnp.zeros((256,), jnp.float32)
        return (r_dense_t, ids, tbl_0, tbl_1, tbl_2, tbl_3, tbl_4, tbl_5, tbl_6, tbl_7, tbl_8, tbl_9, tbl_10, tbl_11, tbl_12, tbl_13, tbl_14, tbl_15, tbl_16, tbl_17, tbl_18, tbl_19, tbl_20, tbl_21, tbl_22, tbl_23, tbl_24, tbl_25, W_top1, b_top1, W_top2, b_top2, W_top3)
    r_dense_t, ids, tbl_0, tbl_1, tbl_2, tbl_3, tbl_4, tbl_5, tbl_6, tbl_7, tbl_8, tbl_9, tbl_10, tbl_11, tbl_12, tbl_13, tbl_14, tbl_15, tbl_16, tbl_17, tbl_18, tbl_19, tbl_20, tbl_21, tbl_22, tbl_23, tbl_24, tbl_25, W_top1, b_top1, W_top2, b_top2, W_top3 = _rec_inputs()

    def _L0_rec_setup():
        import jax, jax.numpy as jnp
        import numpy as np
        EPS = 1e-05
        NI = 33
        TRIL_I, TRIL_J = np.tril_indices(NI, k=-1)

        def layer_norm(x, g, b):
            m = jnp.mean(x, axis=-1, keepdims=True)
            v = jnp.mean(jnp.square(x - m), axis=-1, keepdims=True)
            return (x - m) * jax.lax.rsqrt(v + EPS) * g + b
        key = jax.random.key(seed)
        ks = jax.random.split(key, 8)
        B, D_DENSE, N_SP, D_SP = (4096, 256, 26, 64)
        E, PROJ, MAXD, NFLAT = (128, 32, 512, 528)
        dense_t = jax.random.normal(ks[0], (B, D_DENSE), dtype=jnp.float32)
        sparse_t = jax.random.normal(ks[1], (B, N_SP, D_SP), dtype=jnp.float32)
        Wd = jax.random.normal(ks[2], (E, D_DENSE), dtype=jnp.float32) / np.sqrt(D_DENSE)
        Ws = jax.random.normal(ks[3], (E, D_SP), dtype=jnp.float32) / np.sqrt(D_SP)
        Wsi = jax.random.normal(ks[4], (PROJ, N_SP), dtype=jnp.float32) / np.sqrt(N_SP)
        Wl = jax.random.normal(ks[5], (MAXD, NFLAT), dtype=jnp.float32) / np.sqrt(NFLAT)
        gd = jnp.ones((E,), jnp.float32)
        bd = jnp.zeros((E,), jnp.float32)
        gs = jnp.ones((E,), jnp.float32)
        bs = jnp.zeros((E,), jnp.float32)
        gsi = jnp.ones((PROJ,), jnp.float32)
        bsi = jnp.zeros((PROJ,), jnp.float32)
        gl = jnp.ones((MAXD,), jnp.float32)
        bl = jnp.zeros((MAXD,), jnp.float32)
        return {'dense_t': dense_t, 'sparse_t': sparse_t, 'Wd': Wd, 'gd': gd, 'bd': bd, 'Ws': Ws, 'gs': gs, 'bs': bs, 'Wsi': Wsi, 'gsi': gsi, 'bsi': bsi, 'Wl': Wl, 'gl': gl, 'bl': bl, 'dims_in_use': 384}
    _L0_rec_all = _L0_rec_setup()
    _L0_rec_in = {k: v for k, v in _L0_rec_all.items() if k in ('Wd', 'gd', 'bd', 'Ws', 'gs', 'bs', 'Wsi', 'gsi', 'bsi', 'Wl', 'gl', 'bl')}
    del _L0_rec_all
    return {'r_dense_t': r_dense_t, 'ids': ids, 'tbl_0': tbl_0, 'tbl_1': tbl_1, 'tbl_2': tbl_2, 'tbl_3': tbl_3, 'tbl_4': tbl_4, 'tbl_5': tbl_5, 'tbl_6': tbl_6, 'tbl_7': tbl_7, 'tbl_8': tbl_8, 'tbl_9': tbl_9, 'tbl_10': tbl_10, 'tbl_11': tbl_11, 'tbl_12': tbl_12, 'tbl_13': tbl_13, 'tbl_14': tbl_14, 'tbl_15': tbl_15, 'tbl_16': tbl_16, 'tbl_17': tbl_17, 'tbl_18': tbl_18, 'tbl_19': tbl_19, 'tbl_20': tbl_20, 'tbl_21': tbl_21, 'tbl_22': tbl_22, 'tbl_23': tbl_23, 'tbl_24': tbl_24, 'tbl_25': tbl_25, 'W_top1': W_top1, 'b_top1': b_top1, 'W_top2': W_top2, 'b_top2': b_top2, 'W_top3': W_top3, 'L0_rec_Wd': _L0_rec_in['Wd'], 'L0_rec_gd': _L0_rec_in['gd'], 'L0_rec_bd': _L0_rec_in['bd'], 'L0_rec_Ws': _L0_rec_in['Ws'], 'L0_rec_gs': _L0_rec_in['gs'], 'L0_rec_bs': _L0_rec_in['bs'], 'L0_rec_Wsi': _L0_rec_in['Wsi'], 'L0_rec_gsi': _L0_rec_in['gsi'], 'L0_rec_bsi': _L0_rec_in['bsi'], 'L0_rec_Wl': _L0_rec_in['Wl'], 'L0_rec_gl': _L0_rec_in['gl'], 'L0_rec_bl': _L0_rec_in['bl']}

def reference(r_dense_t, ids, tbl_0, tbl_1, tbl_2, tbl_3, tbl_4, tbl_5, tbl_6, tbl_7, tbl_8, tbl_9, tbl_10, tbl_11, tbl_12, tbl_13, tbl_14, tbl_15, tbl_16, tbl_17, tbl_18, tbl_19, tbl_20, tbl_21, tbl_22, tbl_23, tbl_24, tbl_25, W_top1, b_top1, W_top2, b_top2, W_top3, L0_rec_Wd, L0_rec_gd, L0_rec_bd, L0_rec_Ws, L0_rec_gs, L0_rec_bs, L0_rec_Wsi, L0_rec_gsi, L0_rec_bsi, L0_rec_Wl, L0_rec_gl, L0_rec_bl):
    import jax
    import jax.numpy as jnp

    def _L0_rec_ref(dense_t, sparse_t, Wd, gd, bd, Ws, gs, bs, Wsi, gsi, bsi, Wl, gl, bl, dims_in_use):
        import jax, jax.numpy as jnp
        import numpy as np
        EPS = 1e-05
        NI = 33
        TRIL_I, TRIL_J = np.tril_indices(NI, k=-1)

        def layer_norm(x, g, b):
            m = jnp.mean(x, axis=-1, keepdims=True)
            v = jnp.mean(jnp.square(x - m), axis=-1, keepdims=True)
            return (x - m) * jax.lax.rsqrt(v + EPS) * g + b
        x = layer_norm(dense_t @ Wd.T, gd, bd)
        y = layer_norm(jnp.einsum('bnd,ed->bne', sparse_t, Ws), gs, bs)
        y = jnp.einsum('bne,pn->bep', y, Wsi)
        y = layer_norm(y, gsi, bsi)
        y = jnp.swapaxes(y, 1, 2)
        T = jnp.concatenate([x[:, None, :], y], axis=1)
        Z = jnp.einsum('bnd,bmd->bnm', T, T)
        Zflat = Z[:, TRIL_I, TRIL_J]
        out = layer_norm(Zflat @ Wl.T, gl, bl)
        maxd = out.shape[-1]
        mask = (jnp.arange(maxd) < dims_in_use).astype(out.dtype)
        return out * mask
    e = jnp.stack([tbl_0[ids[:, 0]], tbl_1[ids[:, 1]], tbl_2[ids[:, 2]], tbl_3[ids[:, 3]], tbl_4[ids[:, 4]], tbl_5[ids[:, 5]], tbl_6[ids[:, 6]], tbl_7[ids[:, 7]], tbl_8[ids[:, 8]], tbl_9[ids[:, 9]], tbl_10[ids[:, 10]], tbl_11[ids[:, 11]], tbl_12[ids[:, 12]], tbl_13[ids[:, 13]], tbl_14[ids[:, 14]], tbl_15[ids[:, 15]], tbl_16[ids[:, 16]], tbl_17[ids[:, 17]], tbl_18[ids[:, 18]], tbl_19[ids[:, 19]], tbl_20[ids[:, 20]], tbl_21[ids[:, 21]], tbl_22[ids[:, 22]], tbl_23[ids[:, 23]], tbl_24[ids[:, 24]], tbl_25[ids[:, 25]]], axis=1)
    z = _L0_rec_ref(r_dense_t, e, L0_rec_Wd, L0_rec_gd, L0_rec_bd, L0_rec_Ws, L0_rec_gs, L0_rec_bs, L0_rec_Wsi, L0_rec_gsi, L0_rec_bsi, L0_rec_Wl, L0_rec_gl, L0_rec_bl, 384)
    z = z.reshape(z.shape[0], -1)
    h = jnp.concatenate([z, r_dense_t], axis=1)
    h = jnp.maximum(h @ W_top1 + b_top1, 0.0)
    h = jnp.maximum(h @ W_top2 + b_top2, 0.0)
    y = h @ W_top3
    return y

_drawn_inputs = setup_inputs


def setup_inputs(seed=0):
    import zlib

    import numpy as np

    out = dict(_drawn_inputs(seed))
    spreads = {'b_top1': (0.0, 0.1),
     'b_top2': (0.0, 0.1),
     'L0_rec_gd': (1.0, 0.6),
     'L0_rec_bd': (0.0, 0.8),
     'L0_rec_gs': (1.0, 0.6),
     'L0_rec_bs': (0.0, 0.1),
     'L0_rec_gsi': (1.0, 0.2),
     'L0_rec_bsi': (0.0, 0.1),
     'L0_rec_gl': (1.0, 0.2),
     'L0_rec_bl': (0.0, 0.1)}
    factors = {}
    for name, (base, spread) in spreads.items():
        noise = np.random.default_rng([zlib.crc32(name.encode()), seed]).standard_normal(out[name].shape)
        drawn = base * np.exp(spread * noise) if base else spread * noise
        out[name] = jnp.asarray(drawn.astype(out[name].dtype))
    for name, factor in factors.items():
        out[name] = (out[name] * factor).astype(out[name].dtype)
    return out
```

```python
from contextlib import ExitStack

import numpy as np
import concourse.bass as bass
from concourse import mybir

F32 = mybir.dt.float32
BF16 = mybir.dt.bfloat16
I32 = mybir.dt.int32
U32 = mybir.dt.uint32
ALU = mybir.AluOpType
ACT = mybir.ActivationFunctionType
AX = mybir.AxisListType

P = 128
BATCH, NT, D = 512, 26, 64
DENSE, E, PROJ = 256, 128, 32
MAXD, KEEP = 512, 384
F1, F2 = 512, 256
EPS = 1e-5

GROUPS = BATCH // P
HALF = P // 2
CHUNKS = HALF * NT // P
UNITS = 4
UB = HALF // UNITS
UNIT_CHUNKS = [range(0, 4), range(4, 7), range(7, 10), range(10, 13)]
COLS = PROJ + 2
SLOTS = PROJ // 4 + 1
NPAIR = (PROJ + 1) * PROJ // 2
PCH = 5
ZK, DK = KEEP // P, DENSE // P
MT1, MT2 = F1 // P, F2 // P
OT = MAXD // P


def a_pieces():
    out, off = [], 0
    for k in range(UNITS):
        unit = []
        for c in range(CHUNKS):
            lo = max(UB * k, (P * c) // NT)
            hi = min(UB * k + UB - 1, (P * c + P - 1) // NT)
            if lo <= hi:
                unit.append((c, lo, hi, off))
                off += (hi - lo + 1) * PROJ
        out.append(unit)
    return out, off


PIECES, AW = a_pieces()

COL = {}
_at = 0
for _name, _n in (("gd", 1), ("bd", 1), ("gl", ZK), ("bl", ZK), ("b1", MT1), ("b2", MT2), ("w3", MT2),
                  ("grow", 1), ("gcol", SLOTS), ("gI", PCH), ("gJ", PCH), ("hI", PCH), ("hJ", PCH),
                  ("eps", 1), ("one_row", 1), ("m1", 1), ("m2", 1), ("m3", 1), ("n1", 1), ("n2", 1), ("n3", 1)):
    COL[_name] = (_at, _at + _n)
    _at += _n
NCOL = _at


def program(nc, t, out):
    ctx = ExitStack()
    with ctx:
        def sb(name, shape, dt=F32):
            return ctx.enter_context(nc.sbuf_tensor(name, shape, dt))

        def bank(name, shape):
            return ctx.enter_context(nc.psum_tensor(name, shape, F32))

        def sem(name):
            return ctx.enter_context(nc.semaphore(name))

        ids = sb("ids", [P, (GROUPS + 1) * 2 * CHUNKS], I32)
        base = sb("base", [P, 2 * CHUNKS], I32)
        cols = sb("cols", [P, NCOL])
        ident = sb("ident", [P, P])
        wsT = sb("wsT", [P, E])
        gsr = sb("gsr", [P, E])
        bsr = sb("bsr", [P, E])
        blk = sb("blk", [P, P])
        wsi = sb("wsi", [P, PROJ, NT])
        wrow = sb("wrow", [P, CHUNKS, PROJ])
        wbd = sb("wbd", [P, AW])
        mbd = sb("mbd", [P, AW])
        wdT = sb("wdT", [P, DK, E])
        denT = sb("denT", [P, DK, BATCH])
        wf = sb("wf", [P, SLOTS, MAXD])
        wlT = sb("wlT", [P, PCH, MAXD])
        ce = sb("ce", [P, 3, PCH, P])
        w1 = sb("w1", [P, ZK + DK, F1])
        w2 = sb("w2", [P, MT1, F2])
        loads = dict(ids=ids, base=base, cols=cols, ident=ident, wsT=wsT, gsr=gsr, bsr=bsr, blk=blk, wsi=wsi,
                     wrow=wrow, wbd=wbd, mbd=mbd, wdT=wdT, denT=denT, wf=wf, wlT=wlT, ce=ce, w1=w1, w2=w2)
        order = ["ids", "base", "wsT", "ident", "blk", "gsr", "cols", "wrow", "wbd", "mbd", "wsi", "bsr", "wdT",
                 "denT", "wlT", "ce", "wf", "w1", "w2"]

        idx = sb("idx", [P, 2, 2 * CHUNKS], I32)
        mean = sb("mean", [P, 8])
        wsc = sb("wsc", [P, E])
        wse = sb("wse", [P, 2 * D])
        form = sb("form", [P, P])
        ypad = sb("ypad", [P, 2, E])
        nmean = sb("nmean", [P, CHUNKS])
        wdc = sb("wdc", [P, DK, E])
        ones = sb("ones", [P, P])
        ones5 = sb("ones5", [P, P])
        jcol = sb("jcol", [P, PROJ])
        split = sb("split", [P, 3, E], BF16)
        rest = sb("rest", [P, 2, E])
        bias_l = sb("bias_l", [P, E], BF16)
        bias_f = sb("bias_f", [P, E])
        wsum = sb("wsum", [P, PROJ])
        wsuf = sb("wsuf", [P, PROJ])
        bias_r = sb("bias_r", [P, UB, PROJ], BF16)
        xraw = sb("xraw", [P, BATCH])
        xsq = sb("xsq", [P, BATCH])
        xstd = sb("xstd", [P, BATCH])
        xinv = sb("xinv", [P, BATCH])
        xt = sb("xt", [P, BATCH])
        xone = sb("xone", [P, BATCH])
        cm = sb("cm", [P, PCH, P])
        cg = sb("cg", [P, 3, PCH])
        gg = sb("gg", [P, SLOTS])
        fmean = sb("fmean", [P, SLOTS + 1])
        b1c = sb("b1c", [P, MT1])

        emb = sb("emb", [P, CHUNKS, 2, D])
        embT = sb("embT", [P, 4, P])
        prod = sb("prod", [P, 4, P])
        var1 = sb("var1", [P, 8])
        std1 = sb("std1", [P, 8])
        inv1 = sb("inv1", [P, 8])
        embr = sb("embr", [P, CHUNKS, 2, D])
        aT = sb("aT", [P, UB * PROJ])
        sq = [sb(f"sq{h}", [P, UB * PROJ]) for h in range(2)]
        var2 = [sb(f"var2{h}", [P, UB]) for h in range(2)]
        std2 = [sb(f"std2{h}", [P, UB]) for h in range(2)]
        inv2 = [sb(f"inv2{h}", [P, UB]) for h in range(2)]
        u = [sb(f"u{h}", [P, UB, COLS]) for h in range(2)]
        zt = sb("zt", [P, SLOTS, P])
        zsq = sb("zsq", [P, OT, P])
        stdz = sb("stdz", [P, P])
        invz = sb("invz", [P, P])
        zT = sb("zT", [P, ZK, P])
        h1 = sb("h1", [P, MT1, P])
        h2 = sb("h2", [P, MT2, P])
        yrow = sb("yrow", [1, BATCH])

        b_tr = bank("b_tr", [P, 4, P])
        b_t = bank("b_t", [P, 4, P])
        b_a = bank("b_a", [P, 512])
        b_y = [bank(f"b_y{h}", [P, UB * PROJ]) for h in range(2)]
        b_z = bank("b_z", [P, 2, 512])
        b_f = bank("b_f", [P, OT, P])
        bf = b_f[:].rearrange("p a b -> p (a b)")

        loaded = {n: sem(f"loaded_{n}") for n in order}
        gathered = [sem(f"gathered_{c}") for c in range(CHUNKS)]
        idx_ready = sem("idx_ready")
        chunk_free = sem("chunk_free")
        set_up = sem("set_up")
        wsc_ready = sem("wsc_ready")
        wsc_turned = sem("wsc_turned")
        wse_ready = sem("wse_ready")
        square_done = sem("square_done")
        form_ready = sem("form_ready")
        wdc_ready = sem("wdc_ready")
        dense_done = sem("dense_done")
        xraw_ready = sem("xraw_ready")
        xsq_ready = sem("xsq_ready")
        xvar_done = sem("xvar_done")
        xstd_ready = sem("xstd_ready")
        xt_ready = sem("xt_ready")
        ones_ready = sem("ones_ready")
        xsum_done = sem("xsum_done")
        xone_ready = sem("xone_ready")
        wbd_ready = sem("wbd_ready")
        ypad_ready = sem("ypad_ready")
        u_ones = sem("u_ones")
        cm_ready = sem("cm_ready")
        bias_ready = sem("bias_ready")
        sum_rows_done = sem("sum_rows_done")
        sum_rows_ready = sem("sum_rows_ready")
        wf_ready = sem("wf_ready")
        b1_done = sem("b1_done")
        b1_ready = sem("b1_ready")
        emb_turned = sem("emb_turned")
        embT_ready = sem("embT_ready")
        form_done = sem("form_done")
        prod_ready = sem("prod_ready")
        sum1_ready = sem("sum1_ready")
        var1_ready = sem("var1_ready")
        std1_ready = sem("std1_ready")
        inv1_ready = sem("inv1_ready")
        embr_ready = sem("embr_ready")
        a_done = sem("a_done")
        aT_ready = sem("aT_ready")
        y_done = sem("y_done")
        sq_ready = sem("sq_ready")
        var2_ready = sem("var2_ready")
        std2_ready = sem("std2_ready")
        inv2_ready = sem("inv2_ready")
        u_ready = sem("u_ready")
        gram_done = sem("gram_done")
        zt_by_act = sem("zt_by_act")
        zt_by_dve = sem("zt_by_dve")
        pairs_done = sem("pairs_done")
        zsq_ready = sem("zsq_ready")
        zvar_done = sem("zvar_done")
        stdz_ready = sem("stdz_ready")
        invz_ready = sem("invz_ready")
        zT_ready = sem("zT_ready")
        h1_done = sem("h1_done")
        h1_ready = sem("h1_ready")
        h2_done = sem("h2_done")
        h2_ready = sem("h2_ready")
        out_done = sem("out_done")
        yrow_ready = sem("yrow_ready")
        stored = sem("stored")
        block = ctx.enter_context(nc.Block())

        def col(name, i=0, p0=0, p1=P):
            return cols[p0:p1, COL[name][0] + i:COL[name][0] + i + 1]

        def wait(eng, s, value):
            if not isinstance(value, int) or value > 0:
                eng.wait_ge(s, value)

        def upto(s, k):
            return UNITS * s + k + 1

        def walk(eng, slot):
            for k in range(UNITS):
                slot(0, k, True, False)
            with eng.Fori(1, GROUPS) as s:
                for k in range(UNITS):
                    slot(s, k, True, True)
            for k in range(UNITS):
                slot(GROUPS, k, False, True)

        def earlier(s, k, back, cur, prev):
            return (s, k - back, cur) if k >= back else (s - 1, k - back + UNITS, prev)

        def gram_copy(k, h, r):
            q = 32 * (2 * (k % 2) + h)
            n = SLOTS if r < COLS - PROJ else SLOTS - 1
            b0 = HALF * h + UB * k
            src = b_z[q:q + PROJ, :, 0:8 * COLS].rearrange("p t (g c) -> p t g c", c=COLS)[:, :, :, r:r + 4 * (n - 1) + 1:4]
            dst = zt[32 * r:32 * r + PROJ, 0:n, b0:b0 + UB].rearrange("p s (t g) -> p t g s", t=2)
            return dst, src

        @block.sync
        def _(sp):
            for n in order:
                sp.dma_start(loads[n][:], t[n]).then_inc(loaded[n], 16)
            sp.wait_ge(yrow_ready, GROUPS)
            sp.dma_start(out.rearrange("b o -> o b"), yrow[0:1, :]).then_inc(stored, 16)
            sp.wait_ge(stored, 16)

        @block.gpsimd
        def _(pool):
            SPLIT = 7
            NI = 2 * CHUNKS
            pool.wait_ge(loaded["ids"], 16)
            pool.wait_ge(loaded["base"], 16)

            def index(s, late, count):
                lo, hi = (0, 2 * SPLIT) if not late else (2 * SPLIT, NI)
                at = bass.ds(s * NI + lo, hi - lo) if not isinstance(s, int) else slice(s * NI + lo, s * NI + hi)
                nc.gpsimd.tensor_tensor(idx[:, late, lo:hi], ids[:, at], base[:, lo:hi], ALU.add).then_inc(idx_ready, 1)
                pool.wait_ge(idx_ready, count)

            def gather(s, chunks, late):
                for c in chunks:
                    k = next(k for k in range(UNITS) if c in UNIT_CHUNKS[k])
                    if not isinstance(s, int):
                        pool.wait_ge(embr_ready, upto(s - 1, k))
                        pool.sem_inc(chunk_free, 1)
                    for h in range(2):
                        nc.gpsimd.indirect_dma_start(
                            emb[:, c, h, :], None, t["table"],
                            bass.IndirectOffsetOnAxis(ap=idx[:, late, 2 * c + h:2 * c + h + 1].bitcast(U32), axis=0),
                        ).then_inc(gathered[c], 16)

            index(0, 0, 1)
            index(0, 1, 2)
            gather(0, range(SPLIT), 0)
            for c in range(SPLIT):
                pool.wait_ge(gathered[c], 32)
            index(1, 0, 3)
            gather(0, range(SPLIT, CHUNKS), 1)
            with pool.Fori(1, GROUPS) as s:
                gather(s, range(SPLIT), 0)
                for c in range(SPLIT, CHUNKS):
                    pool.wait_ge(gathered[c], 32 * s)
                index(s, 1, 2 * s + 2)
                for c in range(SPLIT):
                    pool.wait_ge(gathered[c], 32 * s + 32)
                index(s + 1, 0, 2 * s + 3)
                gather(s, range(SPLIT, CHUNKS), 1)

        @block.tensor
        def _(pe):
            pe.wait_ge(wsc_ready, 1)
            pe.wait_ge(loaded["ident"], 16)
            nc.tensor.transpose(b_tr[:, 0, :], wsc[:], ident[:]).then_inc(wsc_turned, 1)
            pe.wait_ge(wse_ready, 1)
            nc.tensor.matmul(b_t[:, 0, :], wse[:], wse[:], start=True, stop=True).then_inc(square_done, 1)
            pe.wait_ge(wdc_ready, 1)
            for i in range(DK):
                mm = nc.tensor.matmul(bf, wdc[:, i, :], denT[:, i, :], start=(i == 0), stop=(i == DK - 1))
            mm.then_inc(dense_done, 1)
            pe.wait_ge(ones_ready, 1)
            pe.wait_ge(xsq_ready, 1)
            nc.tensor.matmul(b_y[0][:], ones[:], xsq[:], start=True, stop=True).then_inc(xvar_done, 1)
            pe.wait_ge(xt_ready, 1)
            nc.tensor.matmul(b_y[1][64:96, :], jcol[:], xt[:], start=True, stop=True).then_inc(xsum_done, 1)
            pe.wait_ge(form_ready, 1)

            def constants():
                pe.wait_ge(cm_ready, 1)
                pe.wait_ge(loaded["wlT"], 16)
                for c in range(PCH):
                    mm = nc.tensor.matmul(bf, cm[:, c, :], wlT[:, c, :], start=(c == 0), stop=(c == PCH - 1))
                mm.then_inc(sum_rows_done, 1)
                pe.wait_ge(loaded["w1"], 16)
                pe.wait_ge(sum_rows_ready, 1)
                for m in range(MT1):
                    for i in range(ZK):
                        mm = nc.tensor.matmul(b_f[:, m, 0:1], w1[:, i, P * m:P * m + P], col("bl", i), start=(i == 0), stop=(i == ZK - 1))
                mm.then_inc(b1_done, 1)

            def slot(s, k, cur, prev):
                if cur:
                    wait(pe, embT_ready, upto(s, k) - 1)
                    for i, c in enumerate(UNIT_CHUNKS[k]):
                        pe.wait_ge(gathered[c], 32 * (s + 1))
                        mm = nc.tensor.transpose(b_tr[:, i, :], emb[:, c].rearrange("p h d -> p (h d)"), ident[:])
                    mm.then_inc(emb_turned, 1)
                ms, mk, m_on = earlier(s, k, 1, cur, prev)
                if m_on:
                    if not prev and k == 1:
                        pe.wait_ge(wbd_ready, 1)
                    pe.wait_ge(embr_ready, upto(ms, mk))
                    for i, (c, lo, hi, off) in enumerate(PIECES[mk]):
                        w = (hi - lo + 1) * PROJ
                        o = (lo - UB * mk) * PROJ
                        mm = nc.tensor.matmul(b_a[:, o:o + w], embr[:, c].rearrange("p h d -> p (h d)"), wbd[:, off:off + w],
                                              start=(i == 0), stop=(i == len(PIECES[mk]) - 1), skip_group_check=True)
                    mm.then_inc(a_done, 1)
                gs_, gk, g_on = earlier(s, k, 2, cur, prev)
                if g_on:
                    pe.wait_ge(u_ready, 4 * upto(gs_, gk))
                    wait(pe, zt_by_act, upto(gs_, gk) - 2)
                    wait(pe, zt_by_dve, upto(gs_, gk) - 2)
                    for g in range(UB):
                        for h in range(2):
                            q = 32 * (2 * (gk % 2) + h)
                            mm = nc.tensor.matmul(b_z[q:q + PROJ, g // 8, COLS * (g % 8):COLS * (g % 8) + COLS],
                                                  u[h][:, g, 0:PROJ], u[h][:, g, :], start=True, stop=True)
                    mm.then_inc(gram_done, 1)
                if cur:
                    pe.wait_ge(embT_ready, upto(s, k))
                    wait(pe, prod_ready, upto(s, k) - 1)
                    for i, c in enumerate(UNIT_CHUNKS[k]):
                        mm = nc.tensor.matmul(b_t[:, i, :], embT[:, i, :], form[:], start=True, stop=True)
                    mm.then_inc(form_done, 1)
                if prev and k == 2:
                    pe.wait_ge(zsq_ready, s)
                    for o in range(OT):
                        mm = nc.tensor.matmul(b_tr[:, 0, :], ones5[:], zsq[:, o, :], start=(o == 0), stop=(o == OT - 1))
                    mm.then_inc(zvar_done, 1)
                if prev and k == 3:
                    pe.wait_ge(h1_ready, s)
                    for m in range(MT2):
                        for i in range(MT1):
                            mm = nc.tensor.matmul(b_tr[:, m, :], w2[:, i, P * m:P * m + P], h1[:, i, :], start=(i == 0), stop=(i == MT1 - 1))
                    mm.then_inc(h2_done, 1)
                if m_on:
                    if not prev and k == 1:
                        pe.wait_ge(ypad_ready, 1)
                        pe.wait_ge(bias_ready, 1)
                        pe.wait_ge(xone_ready, 1)
                    pe.wait_ge(aT_ready, upto(ms, mk))
                    for h in range(2):
                        nc.tensor.matmul(b_y[h][:], ypad[:, h, :], aT[:], start=True, stop=False)
                        nc.tensor.matmul(b_y[h][:], bias_l[:], bias_r[:].rearrange("p a b -> p (a b)"), start=False, stop=True).then_inc(y_done, 1)
                if cur and not prev and k == 3:
                    constants()
                if prev and k == 1:
                    pe.wait_ge(zt_by_act, UNITS * s)
                    pe.wait_ge(zt_by_dve, UNITS * s)
                    pe.wait_ge(wf_ready, 1)
                    pe.wait_ge(b1_ready, 1)
                    for o in range(OT):
                        for i in range(SLOTS):
                            mm = nc.tensor.matmul(b_f[:, o, :], wf[:, i, P * o:P * o + P], zt[:, i, :], start=(i == 0), stop=(i == SLOTS - 1))
                    mm.then_inc(pairs_done, 1)
                if prev and k == 2:
                    pe.wait_ge(loaded["w1"], 16)
                    pe.wait_ge(zT_ready, s)
                    at = slice(P * (s - 1), P * s) if isinstance(s, int) else bass.ds(P * (s - 1), P)
                    for m in range(MT1):
                        for i in range(DK):
                            nc.tensor.matmul(b_f[:, m, :], w1[:, ZK + i, P * m:P * m + P], denT[:, i, at], start=(i == 0), stop=False)
                        for i in range(ZK):
                            mm = nc.tensor.matmul(b_f[:, m, :], w1[:, i, P * m:P * m + P], zT[:, i, :], start=False, stop=(i == ZK - 1))
                    mm.then_inc(h1_done, 1)
                if prev and k == 3:
                    pe.wait_ge(h2_ready, s)
                    for i in range(MT2):
                        mm = nc.tensor.matmul(b_a[0:1, 0:P], col("w3", i), h2[:, i, :], start=(i == 0), stop=(i == MT2 - 1))
                    mm.then_inc(out_done, 1)
                    pe.wait_ge(yrow_ready, s)

            pe.wait_ge(loaded["w2"], 16)
            walk(pe, slot)

        @block.scalar
        def _(act):
            act.wait_ge(loaded["cols"], 16)
            act.wait_ge(wsc_turned, 1)
            nc.scalar.copy(wse[:], b_tr[:, 0, :]).then_inc(wse_ready, 1)
            act.wait_ge(dense_done, 1)
            nc.scalar.copy(xraw[:], bf).then_inc(xraw_ready, 1)
            nc.scalar.activation(xsq[:], bf, ACT.Square).then_inc(xsq_ready, 1)
            act.wait_ge(xvar_done, 1)
            nc.scalar.activation(xstd[:], b_y[0][:], ACT.Sqrt, bias=col("eps")).then_inc(xstd_ready, 1)

            def slot(s, k, cur, prev):
                ms, mk, m_on = earlier(s, k, 1, cur, prev)
                gs_, gk, g_on = earlier(s, k, 2, cur, prev)
                if cur:
                    n = len(UNIT_CHUNKS[k])
                    act.wait_ge(emb_turned, upto(s, k))
                    nc.scalar.copy(embT[:, 0:n, :], b_tr[:, 0:n, :]).then_inc(embT_ready, 1)
                if m_on:
                    act.wait_ge(a_done, upto(ms, mk))
                    nc.scalar.copy(aT[:], b_a[:]).then_inc(aT_ready, 1)
                if g_on:
                    act.wait_ge(gram_done, upto(gs_, gk))
                    if gk == 0 and (not isinstance(gs_, int) or gs_ > 0):
                        act.wait_ge(pairs_done, gs_)
                    for r in range(4):
                        ins = nc.scalar.copy(*gram_copy(gk, 0, r))
                    ins.then_inc(zt_by_act, 1)
                if cur:
                    n = 2 * len(UNIT_CHUNKS[k])
                    act.wait_ge(var1_ready, upto(s, k))
                    nc.scalar.activation(std1[:, 0:n], var1[:, 0:n], ACT.Sqrt).then_inc(std1_ready, 1)
                if prev and k == 3:
                    act.wait_ge(h2_done, s)
                    for m in range(MT2):
                        ins = nc.scalar.activation(h2[:, m, :], b_tr[:, m, :], ACT.Relu, bias=col("b2", m))
                    ins.then_inc(h2_ready, 1)
                if prev and k == 2:
                    act.wait_ge(zvar_done, s)
                    nc.scalar.activation(stdz[:], b_tr[:, 0, :], ACT.Sqrt, bias=col("eps")).then_inc(stdz_ready, 1)
                if m_on:
                    for h in range(2):
                        act.wait_ge(y_done, 2 * upto(ms, mk) - 1 + h)
                        nc.scalar.activation(sq[h][:], b_y[h][:], ACT.Square).then_inc(sq_ready, 1)
                    for h in range(2):
                        act.wait_ge(var2_ready, 2 * upto(ms, mk) - 1 + h)
                        nc.scalar.activation(std2[h][:], var2[h][:], ACT.Sqrt, scale=1.0 / PROJ, bias=col("eps")).then_inc(std2_ready, 1)
                if prev and k == 1:
                    act.wait_ge(pairs_done, s)
                    nc.scalar.activation(zsq[:], b_f[:], ACT.Square).then_inc(zsq_ready, 1)
                if prev and k == 2:
                    act.wait_ge(h1_done, s)
                    act.wait_ge(b1_ready, 1)
                    for m in range(MT1):
                        ins = nc.scalar.activation(h1[:, m, :], b_f[:, m, :], ACT.Relu, bias=b1c[:, m:m + 1])
                    ins.then_inc(h1_ready, 1)

            walk(act, slot)

        @block.vector
        def _(dve):
            step = [0]

            def done(ins):
                step[0] += 1
                ins.then_inc(set_up, 1)
                dve.wait_ge(set_up, step[0])

            def ready(ins, s):
                ins.then_inc(s, 1)
                dve.wait_ge(s, 1)

            v = nc.vector
            dve.wait_ge(loaded["wsT"], 16)
            done(v.tensor_reduce(mean[:, 0:1], wsT[:], AX.X, ALU.add))
            done(v.tensor_scalar(mean[:, 1:2], mean[:, 0:1], -1.0 / E, None, ALU.mult))
            ready(v.tensor_scalar(wsc[:], wsT[:], mean[:, 1:2], None, ALU.add), wsc_ready)
            v.memset(ones[:], 1.0 / P)
            v.memset(ones5[:], 1.0 / MAXD)
            v.memset(zt[:], 0.0)
            done(v.memset(jcol[:], 0.0))
            ready(v.memset(jcol[:, 0:1], 1.0), ones_ready)
            for h in range(2):
                v.memset(u[h][:, :, PROJ + 1], 1.0)
            dve.wait_ge(loaded["gsr"], 16)
            done(v.memset(ypad[:], 0.0))
            for h in range(2):
                ins = v.tensor_tensor(ypad[64 * h:64 * h + 64, h, :], wsc[64 * h:64 * h + 64, :], gsr[64 * h:64 * h + 64, :], ALU.mult)
            ready(ins, ypad_ready)
            dve.wait_ge(loaded["blk"], 16)
            dve.wait_ge(square_done, 1)
            ready(v.scalar_tensor_tensor(out=form[:], in0=b_t[:, 0, :], scalar=1.0 / E, in1=blk[:], op0=ALU.mult, op1=ALU.mult), form_ready)
            dve.wait_ge(loaded["wdT"], 16)
            dve.wait_ge(loaded["denT"], 16)
            done(v.tensor_reduce(mean[:, 2:4], wdT[:], AX.X, ALU.add))
            done(v.tensor_scalar(mean[:, 4:6], mean[:, 2:4], -1.0 / E, None, ALU.mult))
            for i in range(DK):
                ins = v.tensor_scalar(wdc[:, i, :], wdT[:, i, :], mean[:, 4 + i:5 + i], None, ALU.add)
            ready(ins, wdc_ready)
            for n in ("wrow", "wbd", "mbd"):
                dve.wait_ge(loaded[n], 16)
            done(v.tensor_reduce(nmean[:], wrow[:], AX.X, ALU.add))
            done(v.tensor_scalar(nmean[:], nmean[:], -1.0 / PROJ, None, ALU.mult))
            for unit in PIECES:
                for c, lo, hi, off in unit:
                    w = (hi - lo + 1) * PROJ
                    ins = v.scalar_tensor_tensor(out=wbd[:, off:off + w], in0=mbd[:, off:off + w], scalar=nmean[:, c:c + 1],
                                                 in1=wbd[:, off:off + w], op0=ALU.mult, op1=ALU.add)
            ready(ins, wbd_ready)
            dve.wait_ge(xstd_ready, 1)
            dve.wait_ge(loaded["cols"], 16)
            done(v.reciprocal(xinv[:], xstd[:]))
            done(v.scalar_tensor_tensor(out=xinv[:], in0=xraw[:], scalar=col("gd"), in1=xinv[:], op0=ALU.mult, op1=ALU.mult))
            ready(v.tensor_scalar(xt[:], xinv[:], col("bd"), None, ALU.add), xt_ready)
            dve.wait_ge(loaded["bsr"], 16)
            dve.wait_ge(loaded["wsi"], 16)
            done(v.tensor_reduce(wsum[:], wsi[:], AX.X, ALU.add))
            done(v.tensor_reduce(mean[:, 6:7], wsum[:], AX.X, ALU.add))
            done(v.tensor_scalar(mean[:, 7:8], mean[:, 6:7], -1.0 / PROJ, None, ALU.mult))
            done(v.tensor_scalar(wsum[:], wsum[:], mean[:, 7:8], None, ALU.add))
            for src, w, pick, dst in ((bsr, E, "m", bias_f), (wsum, PROJ, "n", wsuf)):
                done(v.tensor_copy(split[:, 0, 0:w], src[:, 0:w]))
                done(v.tensor_tensor(rest[:, 0, 0:w], src[:, 0:w], split[:, 0, 0:w], ALU.subtract))
                done(v.tensor_copy(split[:, 1, 0:w], rest[:, 0, 0:w]))
                done(v.tensor_tensor(rest[:, 1, 0:w], rest[:, 0, 0:w], split[:, 1, 0:w], ALU.subtract))
                done(v.tensor_copy(split[:, 2, 0:w], rest[:, 1, 0:w]))
                done(v.tensor_scalar(dst[:, 0:w], split[:, 0, 0:w], col(pick + "1"), None, ALU.mult))
                for j in (1, 2):
                    done(v.scalar_tensor_tensor(out=dst[:, 0:w], in0=split[:, j, 0:w], scalar=col(f"{pick}{j + 1}"), in1=dst[:, 0:w],
                                                op0=ALU.mult, op1=ALU.add))
            v.tensor_copy(bias_l[:], bias_f[:])
            ready(v.tensor_copy(bias_r[:], wsuf[:].unsqueeze(1).broadcast_to([P, UB, PROJ])), bias_ready)
            dve.wait_ge(xsum_done, 1)
            ready(v.tensor_scalar(xone[64:96, :], b_y[1][64:96, :], col("one_row", 0, 64, 96), None, ALU.add), xone_ready)

            def tile_of(name):
                return cols[:, COL[name][0]:COL[name][1]]

            def sum_coefficients():
                dve.wait_ge(loaded["ce"], 16)
                v.tensor_tensor(cg[:, 0, :], tile_of("gI"), tile_of("hJ"), ALU.mult)
                v.tensor_tensor(cg[:, 1, :], tile_of("gJ"), tile_of("hI"), ALU.mult)
                v.tensor_tensor(cg[:, 2, :], tile_of("hI"), tile_of("hJ"), ALU.mult)
                done(v.tensor_scalar(gg[:], tile_of("gcol"), col("grow"), None, ALU.mult))
                for c in range(PCH):
                    ins = v.tensor_scalar(cm[:, c, :], ce[:, 0, c, :], cg[:, 0, c:c + 1], None, ALU.mult)
                done(ins)
                for j in (1, 2):
                    for c in range(PCH):
                        ins = v.scalar_tensor_tensor(out=cm[:, c, :], in0=ce[:, j, c, :], scalar=cg[:, j, c:c + 1], in1=cm[:, c, :],
                                                     op0=ALU.mult, op1=ALU.add)
                    if j == 1:
                        done(ins)
                ready(ins, cm_ready)

            def pair_rows():
                dve.wait_ge(loaded["wf"], 16)
                for i in range(SLOTS - 1):
                    v.tensor_scalar(wf[:, i, :], wf[:, i, :], gg[:, i:i + 1], None, ALU.mult)
                dve.wait_ge(sum_rows_done, 1)
                ready(v.scalar_tensor_tensor(out=wf[:, SLOTS - 1, :], in0=wf[:, SLOTS - 1, :], scalar=gg[:, SLOTS - 1:SLOTS],
                                             in1=bf, op0=ALU.mult, op1=ALU.add), sum_rows_ready)
                done(v.tensor_reduce(fmean[:, 0:SLOTS], wf[:], AX.X, ALU.add))
                done(v.tensor_scalar(fmean[:, 0:SLOTS], fmean[:, 0:SLOTS], -1.0 / MAXD, None, ALU.mult))
                for i in range(SLOTS):
                    ins = v.tensor_scalar(wf[:, i, :], wf[:, i, :], fmean[:, i:i + 1], None, ALU.add)
                ready(ins, wf_ready)
                dve.wait_ge(b1_done, 1)
                ready(v.tensor_tensor(b1c[:], b_f[:, :, 0], tile_of("b1"), ALU.add), b1_ready)

            def slot(s, k, cur, prev):
                ms, mk, m_on = earlier(s, k, 1, cur, prev)
                gs_, gk, g_on = earlier(s, k, 2, cur, prev)
                if g_on:
                    dve.wait_ge(gram_done, upto(gs_, gk))
                    if gk == 0:
                        if not isinstance(gs_, int) or gs_ > 0:
                            dve.wait_ge(pairs_done, gs_)
                        at = slice(P * gs_, P * gs_ + P) if isinstance(gs_, int) else bass.ds(P * gs_, P)
                        v.tensor_copy(zt[64:96, SLOTS - 1, :], xone[64:96, at])
                    for r in range(4):
                        ins = v.tensor_copy(*gram_copy(gk, 1, r))
                    ins.then_inc(zt_by_dve, 1)
                if cur:
                    c0, n = UNIT_CHUNKS[k][0], len(UNIT_CHUNKS[k])
                    U = upto(s, k)
                    src = emb[:, c0:c0 + n]
                    dve.wait_ge(form_done, U)
                    v.tensor_tensor(prod[:, 0:n, :], b_t[:, 0:n, :], src.rearrange("p c h d -> p c (h d)"), ALU.mult).then_inc(prod_ready, 1)
                    dve.wait_ge(prod_ready, U)
                    v.tensor_reduce(var1[:, 0:2 * n], prod[:, 0:n, :].rearrange("p c (h d) -> p (c h) d", h=2), AX.X, ALU.add).then_inc(sum1_ready, 1)
                    dve.wait_ge(sum1_ready, U)
                    v.tensor_scalar(var1[:, 0:2 * n], var1[:, 0:2 * n], 0.0, EPS, ALU.max, ALU.add).then_inc(var1_ready, 1)
                    dve.wait_ge(std1_ready, U)
                    v.reciprocal(inv1[:, 0:2 * n], std1[:, 0:2 * n]).then_inc(inv1_ready, 1)
                    dve.wait_ge(inv1_ready, U)
                    v.tensor_tensor(embr[:, c0:c0 + n].rearrange("p c h d -> p (c h) d"), src.rearrange("p c h d -> p (c h) d"),
                                    inv1[:, 0:2 * n].unsqueeze(2).broadcast_to([P, 2 * n, D]), ALU.mult).then_inc(embr_ready, 1)
                if prev and k == 2:
                    dve.wait_ge(stdz_ready, s)
                    v.reciprocal(invz[:], stdz[:]).then_inc(invz_ready, 1)
                    dve.wait_ge(invz_ready, s)
                    for i in range(ZK):
                        ins = v.scalar_tensor_tensor(out=zT[:, i, :], in0=b_f[:, i, :], scalar=col("gl", i), in1=invz[:], op0=ALU.mult, op1=ALU.mult)
                    ins.then_inc(zT_ready, 1)
                if m_on:
                    for h in range(2):
                        N = 2 * upto(ms, mk) - 1 + h
                        dve.wait_ge(sq_ready, N)
                        v.tensor_reduce(var2[h][:], sq[h][:].rearrange("p (b q) -> p b q", q=PROJ), AX.X, ALU.add).then_inc(var2_ready, 1)
                    for h in range(2):
                        N = 2 * upto(ms, mk) - 1 + h
                        dve.wait_ge(std2_ready, N)
                        v.reciprocal(inv2[h][:], std2[h][:]).then_inc(inv2_ready, 1)
                        b0 = P * ms + HALF * h + UB * mk
                        at = slice(b0, b0 + UB) if isinstance(ms, int) else bass.ds(b0, UB)
                        v.tensor_copy(u[h][:, :, PROJ], xt[:, at]).then_inc(u_ready, 1)
                        dve.wait_ge(inv2_ready, N)
                        v.tensor_tensor(u[h][:, :, 0:PROJ], b_y[h][:].rearrange("p (b q) -> p b q", q=PROJ),
                                        inv2[h][:].unsqueeze(2).broadcast_to([P, UB, PROJ]), ALU.mult).then_inc(u_ready, 1)
                if cur and not prev and k == 2:
                    sum_coefficients()
                if cur and not prev and k == 3:
                    pair_rows()
                if prev and k == 3:
                    dve.wait_ge(out_done, s)
                    at = slice(P * (s - 1), P * s) if isinstance(s, int) else bass.ds(P * (s - 1), P)
                    v.tensor_copy(yrow[0:1, at], b_a[0:1, 0:P]).then_inc(yrow_ready, 1)

            walk(dve, slot)


def shape_constants():
    rows = [12500, 1000, 12500, 1000, 1000, 1000, 12500, 125000, 1250, 125000, 125000, 1250, 12500, 1250, 12500, 1000,
            1250, 1250, 1250, 12500, 1250, 1250, 1250, 12500, 12500, 1250]
    first = np.concatenate([[0], np.cumsum(rows)[:-1]]).astype(np.int32)
    f = np.arange(CHUNKS * P)
    row_b, row_n = (f // NT).reshape(CHUNKS, P), (f % NT).reshape(CHUNKS, P)
    return first, row_b, row_n


def lay_out(inputs):
    g = {k: np.asarray(v) for k, v in inputs.items()}
    first, row_b, row_n = shape_constants()
    a = {}
    a["table"] = np.concatenate([g[f"tbl_{i}"] for i in range(NT)], axis=0)
    ids = g["ids"].reshape(GROUPS, 2, HALF, NT)
    a["ids"] = np.ascontiguousarray(ids[:, :, row_b, row_n].transpose(3, 0, 2, 1).reshape(P, -1))
    a["ids"] = np.pad(a["ids"], ((0, 0), (0, 2 * CHUNKS)))
    a["base"] = np.ascontiguousarray(np.repeat(first[row_n].T[:, :, None], 2, axis=2).reshape(P, -1))
    a["ident"] = np.eye(P, dtype=np.float32)
    ws, gs, bs = g["L0_rec_Ws"], g["L0_rec_gs"], g["L0_rec_bs"]
    a["wsT"] = np.ascontiguousarray(np.concatenate([ws.T, ws.T], axis=0))
    a["gsr"] = np.ascontiguousarray(np.broadcast_to(gs, (P, E)))
    a["bsr"] = np.ascontiguousarray(np.broadcast_to(bs, (P, E)))
    a["blk"] = np.kron(np.eye(2), np.ones((D, D))).astype(np.float32)
    wsi = g["L0_rec_Wsi"]
    a["wsi"] = np.ascontiguousarray(np.broadcast_to(wsi, (P, PROJ, NT)))
    a["wrow"] = np.ascontiguousarray(wsi.T[row_n].transpose(1, 0, 2))
    wbd, mbd = np.zeros((P, AW), np.float32), np.zeros((P, AW), np.float32)
    for unit in PIECES:
        for c, lo, hi, off in unit:
            for p in range(P):
                b = row_b[c, p]
                if lo <= b <= hi:
                    at = off + (b - lo) * PROJ
                    wbd[p, at:at + PROJ] = wsi[:, row_n[c, p]]
                    mbd[p, at:at + PROJ] = 1.0
    a["wbd"], a["mbd"] = wbd, mbd
    a["wdT"] = np.ascontiguousarray(g["L0_rec_Wd"].T.reshape(DK, P, E).transpose(1, 0, 2))
    a["denT"] = np.ascontiguousarray(g["r_dense_t"].T.reshape(DK, P, BATCH).transpose(1, 0, 2))
    wl, gsi, bsi = g["L0_rec_Wl"], g["L0_rec_gsi"], g["L0_rec_bsi"]
    ti, tj = np.tril_indices(PROJ + 1, k=-1)
    pair = {(int(i), int(j)): n for n, (i, j) in enumerate(zip(ti, tj))}
    wf = np.zeros((4, PROJ, SLOTS, MAXD), np.float32)
    gcol = np.ones((4, PROJ, SLOTS), np.float32)
    for c in range(PROJ):
        s, r = c // 4, c % 4
        gcol[r, :, s] = gsi[c]
        for p in range(c + 1, PROJ):
            wf[r, p, s] = wl[:, pair[p + 1, c + 1]]
    for p in range(PROJ):
        wf[0, p, SLOTS - 1] = wl[:, pair[p + 1, 0]]
    a["wf"] = wf.reshape(P, SLOTS, MAXD)
    wlT = np.zeros((PCH * P, MAXD), np.float32)
    wlT[:NPAIR] = wl.T
    a["wlT"] = np.ascontiguousarray(wlT.reshape(PCH, P, MAXD).transpose(1, 0, 2))
    ce = np.zeros((3, PCH * P, P), np.float32)
    n = np.arange(NPAIR)
    real = tj > 0
    ce[0, n[real], 32 + ti[real] - 1] = 1.0
    ce[1, n[real], 32 + tj[real] - 1] = 1.0
    ce[1, n[~real], 64] = 1.0
    ce[2, n[real], 65] = E
    a["ce"] = np.ascontiguousarray(ce.reshape(3, PCH, P, P).transpose(2, 0, 1, 3))
    w1 = np.concatenate([g["W_top1"][:KEEP], g["W_top1"][MAXD:]], axis=0)
    a["w1"] = np.ascontiguousarray(w1.reshape(ZK + DK, P, F1).transpose(1, 0, 2))
    a["w2"] = np.ascontiguousarray(g["W_top2"].reshape(MT1, P, F2).transpose(1, 0, 2))

    cols = np.zeros((P, NCOL), np.float32)

    def put(name, values):
        cols[:, COL[name][0]:COL[name][1]] = values

    put("gd", g["L0_rec_gd"].reshape(P, 1))
    put("bd", g["L0_rec_bd"].reshape(P, 1))
    put("gl", g["L0_rec_gl"][:KEEP].reshape(ZK, P).T)
    put("bl", g["L0_rec_bl"][:KEEP].reshape(ZK, P).T)
    put("b1", g["b_top1"].reshape(MT1, P).T)
    put("b2", g["b_top2"].reshape(MT2, P).T)
    put("w3", g["W_top3"].reshape(MT2, P).T)
    put("grow", np.tile(gsi, 4).reshape(P, 1))
    put("gcol", gcol.reshape(P, SLOTS))

    def pairs(values, x_value):
        full = np.zeros(PCH * P, np.float32)
        full[:NPAIR] = values
        full[:NPAIR][x_value[0]] = x_value[1]
        return full.reshape(PCH, P).T

    never = np.zeros(NPAIR, bool)
    put("gI", pairs(gsi[ti - 1], (never, 0.0)))
    put("hI", pairs(bsi[ti - 1], (never, 0.0)))
    put("gJ", pairs(gsi[np.maximum(tj, 1) - 1], (~real, 1.0)))
    put("hJ", pairs(bsi[np.maximum(tj, 1) - 1], (~real, 0.0)))
    put("eps", EPS)
    cols[65, COL["one_row"][0]] = 1.0
    for i in range(3):
        for j in range(3):
            cols[3 * i + j, COL[f"m{i + 1}"][0]] = 1.0
            cols[3 * i + j, COL[f"n{j + 1}"][0]] = 1.0
    a["cols"] = cols
    return a


def kernel(**inputs):
    import concourse.bacc as _bacc
    from concourse.bass_utils import run_bass_kernel_spmd as _run

    arrays = lay_out(inputs)
    nc = _bacc.Bacc("TRN2", target_bir_lowering=False, num_devices=1)
    t = {n: nc.dram_tensor("in_" + n, v.shape, mybir.dt.from_np(v.dtype), kind="ExternalInput").ap() for n, v in arrays.items()}
    out = nc.dram_tensor("out", (BATCH, 1), F32, kind="ExternalOutput").ap()
    program(nc, t, out)
    r = _run(nc, [{"in_" + n: v for n, v in arrays.items()}], core_ids=[0])
    return r.results[0]["out"]
```

```python
from contextlib import ExitStack

import numpy as np
import concourse.bass as bass
from concourse import mybir

F32 = mybir.dt.float32
BF16 = mybir.dt.bfloat16
I32 = mybir.dt.int32
U32 = mybir.dt.uint32
ALU = mybir.AluOpType
ACT = mybir.ActivationFunctionType
AX = mybir.AxisListType

P = 128
BATCH, NT, D = 512, 26, 64
DENSE, E, PROJ = 256, 128, 32
MAXD, KEEP = 512, 384
F1, F2 = 512, 256
EPS = 1e-5

GROUPS = BATCH // P
HALF = P // 2
CHUNKS = HALF * NT // P
UNITS = 4
UB = HALF // UNITS
UNIT_CHUNKS = [range(0, 4), range(4, 7), range(7, 10), range(10, 13)]
COLS = PROJ + 2
SQ = PROJ // 8
SLOTS = PROJ // 4 + 1
LAST = SLOTS - 1
PAIR_SLOTS = [*range(SQ), LAST]
WS = len(PAIR_SLOTS)
SUMS = PROJ + COLS
NPAIR = (PROJ + 1) * PROJ // 2
PCH = 5
ZK, DK = KEEP // P, DENSE // P
MT1, MT2 = F1 // P, F2 // P
OT = MAXD // P


def a_pieces():
    out, off = [], 0
    for k in range(UNITS):
        unit = []
        for c in range(CHUNKS):
            lo = max(UB * k, (P * c) // NT)
            hi = min(UB * k + UB - 1, (P * c + P - 1) // NT)
            if lo <= hi:
                unit.append((c, lo, hi, off))
                off += hi - lo + 1
        out.append(unit)
    return out, off


PIECES, AB = a_pieces()

COL = {}
NCOL = 0
for _name, _n in (("wsT", E), ("ident", P), ("blk", P), ("eps", 1), ("gsr", E), ("gd", 1), ("bd", 1), ("gl", ZK),
                  ("bl", ZK), ("b1", MT1), ("b2", MT2), ("w3", MT2), ("grow", WS), ("gcol", WS), ("gI", PCH),
                  ("gJ", PCH), ("hI", PCH), ("hJ", PCH), ("one_row", 1), ("moved", SQ), ("own", AB),
                  ("wrow", CHUNKS * PROJ)):
    COL[_name] = (NCOL, NCOL + _n)
    NCOL += _n
PARTS = 3
BCOL = {}
NBCOL = 0
for _name, _n in (("bs", E), ("pick_bs", PARTS), ("pick_ws", PARTS), ("wsi", PROJ * NT)):
    BCOL[_name] = (NBCOL, NBCOL + _n)
    NBCOL += _n


def program(nc, t, out):
    ctx = ExitStack()
    with ctx:
        def sb(name, shape, dt=F32):
            return ctx.enter_context(nc.sbuf_tensor(name, shape, dt))

        def bank(name, shape):
            return ctx.enter_context(nc.psum_tensor(name, shape, F32))

        def sem(name):
            return ctx.enter_context(nc.semaphore(name))

        ids = sb("ids", [P, (GROUPS + 2) * 2 * CHUNKS], I32)
        cols = sb("cols", [P, NCOL])
        bcols = sb("bcols", [PARTS * PARTS, NBCOL])
        wdT = sb("wdT", [P, DK, E])
        denT = sb("denT", [P, DK, BATCH])
        w1d = sb("w1d", [P, DK, F1])
        w1z = sb("w1z", [P, ZK, F1])
        wf = sb("wf", [P, WS, MAXD])
        wlT = sb("wlT", [P, PCH, MAXD])
        ce = sb("ce", [P, 3, PCH, SUMS])
        w2 = sb("w2", [P, MT1, F2])
        loads = dict(ids=ids, cols=cols, late_cols=cols, bcols=bcols, wdT=wdT, denT=denT, w1d=w1d, w1z=w1z, wf=wf, wlT=wlT, ce=ce, w2=w2)
        early = COL["gsr"][0]
        first_loads = [("ids", [slice(None)]), ("cols", [slice(0, early)]), ("wdT", [slice(None)]), ("denT", [0, 1]),
                       ("late_cols", [slice(early, NCOL)]), ("w1d", [0, 1]), ("bcols", [slice(None)])]
        later_loads = [("ce", range(3)), ("wlT", range(PCH)), ("wf", range(WS)), ("w1z", range(ZK)),
                       ("w2", [slice(0, 2), slice(2, 4)])]
        count = {name: 16 * len(parts) for name, parts in first_loads + later_loads}

        def of(name):
            return cols[:, COL[name][0]:COL[name][1]]

        def col(name, i=0, p0=0, p1=P):
            return cols[p0:p1, COL[name][0] + i:COL[name][0] + i + 1]

        def bof(name):
            return bcols[:, BCOL[name][0]:BCOL[name][1]]

        ident = of("ident")
        base = ids[:, (GROUPS + 1) * 2 * CHUNKS:(GROUPS + 2) * 2 * CHUNKS]

        idx = sb("idx", [P, 2, 2 * CHUNKS], I32)
        mean = sb("mean", [P, 8])
        wsc = sb("wsc", [P, E])
        wse = sb("wse", [P, 2 * D])
        form = sb("form", [P, P])
        ypad = sb("ypad", [P, 2, E])
        nmean = sb("nmean", [P, CHUNKS])
        wcen = sb("wcen", [P, CHUNKS, PROJ])
        wbd = sb("wbd", [P, AB, PROJ])
        wdc = sb("wdc", [P, DK, E])
        jcol = sb("jcol", [P, PROJ])
        R9 = PARTS * PARTS
        whole = sb("whole", [R9, E + PROJ])
        split = sb("split", [R9, PARTS, E + PROJ], BF16)
        rest = sb("rest", [R9, 2, E + PROJ])
        bmean = sb("bmean", [R9, 2])
        bias_l = sb("bias_l", [P, E], BF16)
        picked = sb("picked", [R9, PROJ], BF16)
        bias_r = sb("bias_r", [P, UB, PROJ], BF16)
        xsq = sb("xsq", [P, GROUPS, E])
        xvar = sb("xvar", [P, GROUPS])
        xstd = sb("xstd", [P, GROUPS])
        xinv = sb("xinv", [P, GROUPS])
        xn = sb("xn", [P, GROUPS, E])
        xt = sb("xt", [P, BATCH])
        xone = sb("xone", [P, BATCH])
        dd = sb("dd", [P, MT1, BATCH])
        cm = sb("cm", [P, PCH, SUMS])
        cg = sb("cg", [P, 3, PCH])
        gg = sb("gg", [P, WS])
        fsum = sb("fsum", [P, WS])
        fmean = sb("fmean", [P, WS])

        emb = sb("emb", [P, CHUNKS, 2, D])
        embT = sb("embT", [P, 4, P])
        prod = sb("prod", [P, 4, P])
        var1 = sb("var1", [P, 8])
        std1 = sb("std1", [P, 8])
        inv1 = sb("inv1", [P, 8])
        embr = sb("embr", [P, CHUNKS, 2, D])
        aT = sb("aT", [P, UB * PROJ])
        sq = [sb(f"sq{h}", [P, UB * PROJ]) for h in range(2)]
        var2 = [sb(f"var2{h}", [P, UB]) for h in range(2)]
        std2 = [sb(f"std2{h}", [P, UB]) for h in range(2)]
        inv2 = [sb(f"inv2{h}", [P, UB]) for h in range(2)]
        u = [[sb(f"u{k}{h}", [P, UB, COLS]) for h in range(2)] for k in range(2)]
        zt = sb("zt", [P, SLOTS, P])
        zsq = sb("zsq", [P, MAXD])
        varz = sb("varz", [P, 1])
        stdz = sb("stdz", [P, 1])
        invz = sb("invz", [P, 1])
        zn = sb("zn", [P, KEEP])
        zT = sb("zT", [P, ZK, P])
        h1s = sb("h1s", [P, MT1, P])
        h1 = sb("h1", [P, MT1, P])
        h2 = sb("h2", [P, MT2, P])
        yrow = sb("yrow", [1, BATCH])
        first_root = sb("first_root", [P, 1])

        b_tr = bank("b_tr", [P, 4, P])
        b_t = bank("b_t", [P, 4, P])
        b_a = bank("b_a", [P, 512])
        b_y = [bank(f"b_y{h}", [P, UB * PROJ]) for h in range(2)]
        b_z = bank("b_z", [P, 2, 512])
        b_f = bank("b_f", [P, OT, P])
        dd_banks = [b_y[0][:], b_y[1][:], b_z[:, 0, :], b_z[:, 1, :]]
        h1_banks = [b_tr, b_f]
        bf = b_f[:].rearrange("p a b -> p (a b)")

        loaded = {n: sem(f"loaded_{n}") for n in count}
        gathered = [sem(f"gathered_{c}") for c in range(CHUNKS)]
        idx_ready = sem("idx_ready")
        chunk_free = sem("chunk_free")
        set_up = sem("set_up")
        wsc_ready = sem("wsc_ready")
        wsc_turned = sem("wsc_turned")
        wse_ready = sem("wse_ready")
        square_done = sem("square_done")
        form_ready = sem("form_ready")
        wdc_ready = sem("wdc_ready")
        dense_done = sem("dense_done")
        xvar_ready = sem("xvar_ready")
        xstd_ready = sem("xstd_ready")
        xn_ready = sem("xn_ready")
        x_turned = sem("x_turned")
        xt_ready = sem("xt_ready")
        tiles_cleared = sem("tiles_cleared")
        tiles_set = sem("tiles_set")
        xsum_done = sem("xsum_done")
        xone_ready = sem("xone_ready")
        wbd_ready = sem("wbd_ready")
        ypad_ready = sem("ypad_ready")
        u_ones = sem("u_ones")
        cm_ready = sem("cm_ready")
        bs_placed = sem("bs_placed")
        bias_ready = sem("bias_ready")
        sum_rows_done = sem("sum_rows_done")
        sum_rows_ready = sem("sum_rows_ready")
        wf_ready = sem("wf_ready")
        wf_scaled = sem("wf_scaled")
        fmean_ready = sem("fmean_ready")
        gg_ready = sem("gg_ready")
        dd_done = sem("dd_done")
        dd_ready = sem("dd_ready")
        emb_turned = sem("emb_turned")
        embT_ready = sem("embT_ready")
        form_done = sem("form_done")
        prod_ready = sem("prod_ready")
        sum1_ready = sem("sum1_ready")
        var1_ready = sem("var1_ready")
        std1_ready = sem("std1_ready")
        inv1_ready = sem("inv1_ready")
        embr_ready = sem("embr_ready")
        a_done = sem("a_done")
        aT_ready = sem("aT_ready")
        y_done = sem("y_done")
        sq_ready = sem("sq_ready")
        var2_ready = sem("var2_ready")
        std2_ready = sem("std2_ready")
        inv2_ready = sem("inv2_ready")
        u_ready = sem("u_ready")
        gram_done = sem("gram_done")
        zt_ready = sem("zt_ready")
        zt_x_ready = sem("zt_x_ready")
        pairs_done = sem("pairs_done")
        zt_seen = sem("zt_seen")
        zt_moved = sem("zt_moved")
        move_seen = sem("move_seen")
        zt_packed = sem("zt_packed")
        varz_ready = sem("varz_ready")
        stdz_ready = sem("stdz_ready")
        invz_ready = sem("invz_ready")
        zn_ready = sem("zn_ready")
        z_turned = sem("z_turned")
        zT_ready = sem("zT_ready")
        h1_summed = sem("h1_summed")
        h1_done = sem("h1_done")
        h1_ready = sem("h1_ready")
        h2_done = sem("h2_done")
        h2_ready = sem("h2_ready")
        out_done = sem("out_done")
        yrow_ready = sem("yrow_ready")
        stored = sem("stored")
        block = ctx.enter_context(nc.Block())

        def wait(eng, s, value):
            if not isinstance(value, int) or value > 0:
                eng.wait_ge(s, value)

        def upto(s, k):
            return UNITS * s + k + 1

        def walk(eng, slot, after_first=None):
            for k in range(UNITS):
                slot(0, k, True, False)
            if after_first:
                after_first()
            with eng.Fori(1, GROUPS) as s:
                for k in range(UNITS):
                    slot(s, k, True, True)
            for k in range(UNITS):
                slot(GROUPS, k, False, True)

        def earlier(s, k, back, cur, prev):
            return (s, k - back, cur) if k >= back else (s - 1, k - back + UNITS, prev)

        def gram_copy(k, h, r):
            q = 32 * (2 * (k % 2) + h)
            n = SLOTS if r < COLS - PROJ else SLOTS - 1
            b0 = HALF * h + UB * k
            src = b_z[q:q + PROJ, :, 0:8 * COLS].rearrange("p t (g c) -> p t g c", c=COLS)[:, :, :, r:r + 4 * (n - 1) + 1:4]
            dst = zt[32 * r:32 * r + PROJ, 0:n, b0:b0 + UB].rearrange("p s (t g) -> p t g s", t=2)
            return dst, src

        @block.sync
        def _(sp):
            for n, parts in first_loads:
                for part in parts:
                    src = t["cols" if n == "late_cols" else n]
                    sp.dma_start(loads[n][:, part], src[:, part]).then_inc(loaded[n], 16)
            later = [(n, part) for n, parts in later_loads for part in parts]
            for i, (n, part) in enumerate(later):
                if i % 2 == 0:
                    sp.wait_ge(gathered[i // 2], 32)
                sp.dma_start(loads[n][:, part], t[n][:, part]).then_inc(loaded[n], 16)
            sp.wait_ge(yrow_ready, GROUPS + 1)
            sp.dma_start(out.rearrange("b o -> o b"), yrow[0:1, :]).then_inc(stored, 16)
            sp.wait_ge(stored, 16)

        @block.gpsimd
        def _(pool):
            SPLIT = 7
            NI = 2 * CHUNKS
            for tile in (ypad[:], bias_l[:], bias_r[:], jcol[:], zt[:, LAST, :]):
                nc.gpsimd.memset(tile, 0.0).then_inc(tiles_cleared, 1)
            pool.wait_ge(tiles_cleared, 5)
            nc.gpsimd.memset(jcol[:, 0:1], 1.0).then_inc(tiles_set, 1)
            nc.gpsimd.memset(yrow[:], 0.0).then_inc(yrow_ready, 1)
            for k in range(2):
                for h in range(2):
                    nc.gpsimd.memset(u[k][h][:, :, PROJ + 1], 1.0).then_inc(tiles_set, 1)
            pool.wait_ge(loaded["ids"], count["ids"])

            def index(s, late, count):
                lo, hi = (0, 2 * SPLIT) if not late else (2 * SPLIT, NI)
                at = bass.ds(s * NI + lo, hi - lo) if not isinstance(s, int) else slice(s * NI + lo, s * NI + hi)
                nc.gpsimd.tensor_tensor(idx[:, late, lo:hi], ids[:, at], base[:, lo:hi], ALU.add).then_inc(idx_ready, 1)
                pool.wait_ge(idx_ready, count)

            def gather(s, chunks, late):
                for c in chunks:
                    k = next(k for k in range(UNITS) if c in UNIT_CHUNKS[k])
                    if not isinstance(s, int):
                        pool.wait_ge(embr_ready, upto(s - 1, k))
                        pool.sem_inc(chunk_free, 1)
                    for h in range(2):
                        nc.gpsimd.indirect_dma_start(
                            emb[:, c, h, :], None, t["table"],
                            bass.IndirectOffsetOnAxis(ap=idx[:, late, 2 * c + h:2 * c + h + 1].bitcast(U32), axis=0),
                        ).then_inc(gathered[c], 16)

            index(0, 0, 1)
            index(0, 1, 2)
            gather(0, range(SPLIT), 0)
            gather(0, range(SPLIT, CHUNKS), 1)
            for c in range(SPLIT):
                pool.wait_ge(gathered[c], 32)
            index(1, 0, 3)
            with pool.Fori(1, GROUPS) as s:
                gather(s, range(SPLIT), 0)
                for c in range(SPLIT, CHUNKS):
                    pool.wait_ge(gathered[c], 32 * s)
                index(s, 1, 2 * s + 2)
                gather(s, range(SPLIT, CHUNKS), 1)
                for c in range(SPLIT):
                    pool.wait_ge(gathered[c], 32 * s + 32)
                index(s + 1, 0, 2 * s + 3)

        @block.tensor
        def _(pe):
            pe.wait_ge(wsc_ready, 1)
            nc.tensor.transpose(b_tr[:, 0, :], wsc[:], ident).then_inc(wsc_turned, 1)
            pe.wait_ge(wse_ready, 1)
            nc.tensor.matmul(b_t[:, 0, :], wse[:], wse[:], start=True, stop=True).then_inc(square_done, 1)
            pe.wait_ge(form_ready, 1)

            def dense_product():
                pe.wait_ge(wdc_ready, 1)
                pe.wait_ge(loaded["denT"], count["denT"])
                for g in range(GROUPS):
                    for i in range(DK):
                        mm = nc.tensor.matmul(b_f[:, g, :], denT[:, i, P * g:P * g + P], wdc[:, i, :], start=(i == 0), stop=(i == DK - 1))
                mm.then_inc(dense_done, 1)

            def first_layer_dense(blocks):
                pe.wait_ge(loaded["w1d"], count["w1d"])
                for m in blocks:
                    for i in range(DK):
                        mm = nc.tensor.matmul(dd_banks[m], w1d[:, i, P * m:P * m + P], denT[:, i, :], start=(i == 0), stop=(i == DK - 1))
                    mm.then_inc(dd_done, 1)

            def turn_x():
                pe.wait_ge(xn_ready, 1)
                for g in range(GROUPS):
                    mm = nc.tensor.transpose(b_f[:, g, :], xn[:, g, :], ident)
                mm.then_inc(x_turned, 1)

            def sum_x():
                pe.wait_ge(tiles_set, 1)
                pe.wait_ge(xt_ready, 1)
                nc.tensor.matmul(b_a[64:96, :], jcol[:], xt[:], start=True, stop=True).then_inc(xsum_done, 1)

            def sum_rows():
                pe.wait_ge(cm_ready, 1)
                pe.wait_ge(loaded["wlT"], count["wlT"])
                for c in range(PCH):
                    mm = nc.tensor.matmul(bf[0:SUMS], cm[:, c, :], wlT[:, c, :], start=(c == 0), stop=(c == PCH - 1))
                mm.then_inc(sum_rows_done, 1)

            def keep_warm(n):
                for i in range(n):
                    nc.tensor.matmul(b_t[:].rearrange("p a b -> p (a b)"), bias_l[:], bias_r[:].rearrange("p a b -> p (a b)"), start=True, stop=True)

            def gram(s, k, h, prev):
                U = upto(s, k)
                pe.wait_ge(u_ready, 4 * U - 2 + 2 * h)
                if not prev and k == 0 and h == 0:
                    pe.wait_ge(tiles_set, 5)
                    pe.wait_ge(dd_ready, MT1)
                wait(pe, zt_ready, 2 * U - 5 + h)
                q = 32 * (2 * (k % 2) + h)
                uu = u[k % 2][h]
                for g in range(UB):
                    mm = nc.tensor.matmul(b_z[q:q + PROJ, g // 8, COLS * (g % 8):COLS * (g % 8) + COLS],
                                          uu[:, g, 0:PROJ], uu[:, g, :], start=True, stop=True)
                mm.then_inc(gram_done, 1)

            def slot(s, k, cur, prev):
                ms, mk, m_on = earlier(s, k, 1, cur, prev)
                gs_, gk, g_on = earlier(s, k, 2, cur, prev)
                if cur:
                    for i, c in enumerate(UNIT_CHUNKS[k]):
                        pe.wait_ge(gathered[c], 32 * (s + 1))
                        mm = nc.tensor.transpose(b_tr[:, i, :], emb[:, c].rearrange("p h d -> p (h d)"), ident)
                    mm.then_inc(emb_turned, 1)
                if m_on:
                    if not prev and k == 1:
                        pe.wait_ge(wbd_ready, 1)
                        pe.wait_ge(xone_ready, 1)
                    pe.wait_ge(embr_ready, upto(ms, mk))
                    for i, (c, lo, hi, off) in enumerate(PIECES[mk]):
                        nb = hi - lo + 1
                        o = (lo - UB * mk) * PROJ
                        mm = nc.tensor.matmul(b_a[:, o:o + nb * PROJ], embr[:, c].rearrange("p h d -> p (h d)"),
                                              wbd[:, off:off + nb, :].rearrange("p b q -> p (b q)"),
                                              start=(i == 0), stop=(i == len(PIECES[mk]) - 1), skip_group_check=True)
                    mm.then_inc(a_done, 1)
                if prev and k == 3:
                    pe.wait_ge(zn_ready, s)
                    for i in range(ZK):
                        mm = nc.tensor.transpose(b_f[:, i, :], zn[:, P * i:P * i + P], ident)
                    mm.then_inc(z_turned, 1)
                    if not cur:
                        keep_warm(5)
                if cur:
                    pe.wait_ge(embT_ready, upto(s, k))
                    wait(pe, prod_ready, upto(s, k) - 1)
                    for i, c in enumerate(UNIT_CHUNKS[k]):
                        mm = nc.tensor.matmul(b_t[:, i, :], embT[:, i, :], form[:], start=True, stop=True)
                    mm.then_inc(form_done, 1)
                if g_on:
                    gram(gs_, gk, 0, prev)
                if prev and k == 3:
                    pe.wait_ge(loaded["w1z"], count["w1z"])
                    pe.wait_ge(zT_ready, ZK * s)
                    for m in range(MT1):
                        for i in range(ZK):
                            mm = nc.tensor.matmul(h1_banks[m // 2][:, m, :], w1z[:, i, P * m:P * m + P], zT[:, i, :], start=(i == 0), stop=(i == ZK - 1))
                        if m % 2 == 1:
                            mm.then_inc(h1_done, 1)
                    if not cur:
                        keep_warm(5)
                if m_on:
                    if not prev and k == 1:
                        pe.wait_ge(ypad_ready, 1)
                        pe.wait_ge(bias_ready, 1)
                        pe.wait_ge(tiles_set, 1)
                        pe.wait_ge(dd_ready, 2)
                    pe.wait_ge(aT_ready, upto(ms, mk))
                    wait(pe, u_ready, 4 * upto(ms, mk) - 4)
                    for h in range(2):
                        nc.tensor.matmul(b_y[h][:], ypad[:, h, :], aT[:], start=True, stop=False)
                        nc.tensor.matmul(b_y[h][:], bias_l[:], bias_r[:].rearrange("p a b -> p (a b)"), start=False, stop=True).then_inc(y_done, 1)
                if prev and k == 2:
                    pe.wait_ge(zt_packed, s)
                    pe.wait_ge(zt_x_ready, s)
                    pe.wait_ge(yrow_ready, s)
                    pe.wait_ge(wf_ready, WS)
                    for i, slot_ in enumerate(PAIR_SLOTS):
                        mm = nc.tensor.matmul(bf, zt[:, slot_, :], wf[:, i, :], start=(i == 0), stop=(i == WS - 1))
                    mm.then_inc(pairs_done, 1)
                    if not cur:
                        keep_warm(8)
                if prev and k == 3:
                    pe.wait_ge(loaded["w2"], count["w2"])
                    pe.wait_ge(h1_ready, 2 * s)
                    for m in range(MT2):
                        for i in range(MT1):
                            mm = nc.tensor.matmul(b_a[:, P * m:P * m + P], w2[:, i, P * m:P * m + P], h1[:, i, :], start=(i == 0), stop=(i == MT1 - 1))
                    mm.then_inc(h2_done, 1)
                if g_on:
                    gram(gs_, gk, 1, prev)
                if not cur and k < 2:
                    keep_warm((8, 12)[k])
                if prev and k == 3:
                    pe.wait_ge(h2_ready, s)
                    for i in range(MT2):
                        mm = nc.tensor.matmul(b_f[0:1, 0, :], col("w3", i), h2[:, i, :], start=(i == 0), stop=(i == MT2 - 1))
                    mm.then_inc(out_done, 1)
                if cur and not prev:
                    if k == 0:
                        sum_x()
                        first_layer_dense([2, 3])
                    if k == 2:
                        sum_rows()

            dense_product()
            first_layer_dense([0, 1])
            turn_x()
            walk(pe, slot)

        @block.scalar
        def _(act):
            act.wait_ge(loaded["cols"], count["cols"])
            nc.scalar.activation(first_root[:], col("eps"), ACT.Sqrt)
            act.wait_ge(wsc_turned, 1)
            nc.scalar.copy(wse[:], b_tr[:, 0, :]).then_inc(wse_ready, 1)

            def x_std():
                act.wait_ge(dense_done, 1)
                for g in range(GROUPS):
                    nc.scalar.activation(xsq[:, g, :], b_f[:, g, :], ACT.Square, accum_out=xvar[:, g:g + 1]).then_inc(xvar_ready, 1)
                act.wait_ge(xvar_ready, GROUPS)
                nc.scalar.activation(xstd[:], xvar[:], ACT.Sqrt, scale=1.0 / E, bias=col("eps")).then_inc(xstd_ready, 1)

            def first_layer_dense(blocks):
                act.wait_ge(loaded["late_cols"], count["late_cols"])
                for m in blocks:
                    act.wait_ge(dd_done, m + 1)
                    nc.scalar.activation(dd[:, m, :], dd_banks[m], ACT.Identity, bias=col("b1", m)).then_inc(dd_ready, 1)

            def x_columns():
                act.wait_ge(x_turned, 1)
                nc.scalar.activation(xt[:], bf, ACT.Identity, scale=col("gd"), bias=col("bd")).then_inc(xt_ready, 1)

            def pair_rows_scale(slots):
                act.wait_ge(loaded["wf"], count["wf"])
                act.wait_ge(gg_ready, 1)
                for i in slots:
                    nc.scalar.activation(wf[:, i, :], wf[:, i, :], ACT.Identity, scale=gg[:, i:i + 1],
                                         accum_out=fsum[:, i:i + 1]).then_inc(wf_scaled, 1)

            def pair_rows_centre(slots):
                act.wait_ge(fmean_ready, 1)
                for i in slots:
                    nc.scalar.activation(wf[:, i, :], wf[:, i, :], ACT.Identity, bias=fmean[:, i:i + 1]).then_inc(wf_ready, 1)

            def copy_gram(s, k, h):
                act.wait_ge(gram_done, 2 * upto(s, k) - 1 + h)
                if k == 0 and h == 0 and (not isinstance(s, int) or s > 0):
                    act.wait_ge(pairs_done, s)
                for r in range(4):
                    ins = nc.scalar.copy(*gram_copy(k, h, r))
                ins.then_inc(zt_ready, 1)

            def second_root(s, k, h):
                act.wait_ge(var2_ready, 2 * upto(s, k) - 1 + h)
                nc.scalar.activation(std2[h][:], var2[h][:], ACT.Sqrt, scale=1.0 / PROJ, bias=col("eps")).then_inc(std2_ready, 1)

            def slot(s, k, cur, prev):
                ms, mk, m_on = earlier(s, k, 1, cur, prev)
                gs_, gk, g_on = earlier(s, k, 2, cur, prev)
                hs, hk, h_on = earlier(s, k, 3, cur, prev)
                if cur:
                    n = len(UNIT_CHUNKS[k])
                    act.wait_ge(emb_turned, upto(s, k))
                    nc.scalar.copy(embT[:, 0:n, :], b_tr[:, 0:n, :]).then_inc(embT_ready, 1)
                if g_on and k != 3:
                    second_root(gs_, gk, 1)
                if m_on:
                    act.wait_ge(a_done, upto(ms, mk))
                    nc.scalar.copy(aT[:], b_a[:]).then_inc(aT_ready, 1)
                if prev and k == 3:
                    act.wait_ge(z_turned, s)
                    for i in range(ZK):
                        nc.scalar.activation(zT[:, i, :], b_f[:, i, :], ACT.Identity, scale=col("gl", i), bias=col("bl", i)).then_inc(zT_ready, 1)
                if h_on and hk == 0:
                    copy_gram(hs, hk, 0)
                    at = slice(P * hs, P * hs + P) if isinstance(hs, int) else bass.ds(P * hs, P)
                    if not prev:
                        act.wait_ge(tiles_set, 1)
                        act.wait_ge(xone_ready, 1)
                    nc.scalar.copy(zt[64:96, LAST, :], xone[64:96, at]).then_inc(zt_x_ready, 1)
                if h_on:
                    copy_gram(hs, hk, 1)
                if g_on and gk > 0:
                    copy_gram(gs_, gk, 0)
                if cur:
                    n = 2 * len(UNIT_CHUNKS[k])
                    act.wait_ge(var1_ready, upto(s, k))
                    nc.scalar.activation(std1[:, 0:n], var1[:, 0:n], ACT.Sqrt).then_inc(std1_ready, 1)
                if prev and k == 3:
                    for m in (0, 2):
                        act.wait_ge(h1_summed, 2 * s - 1 + m // 2)
                        nc.scalar.activation(h1[:, m:m + 2, :], h1s[:, m:m + 2, :], ACT.Relu).then_inc(h1_ready, 1)
                if m_on:
                    for h in range(2):
                        act.wait_ge(y_done, 2 * upto(ms, mk) - 1 + h)
                        nc.scalar.activation(sq[h][:], b_y[h][:], ACT.Square).then_inc(sq_ready, 1)
                    second_root(ms, mk, 0)
                    if k == 2:
                        second_root(ms, mk, 1)
                if prev and k == 2:
                    act.wait_ge(pairs_done, s)
                    nc.scalar.activation(zsq[:], bf, ACT.Square, accum_out=varz[:]).then_inc(varz_ready, 1)
                    act.wait_ge(varz_ready, s)
                    nc.scalar.activation(stdz[:], varz[:], ACT.Sqrt, scale=1.0 / MAXD, bias=col("eps")).then_inc(stdz_ready, 1)
                if prev and k == 3:
                    act.wait_ge(h2_done, s)
                    for m in range(MT2):
                        ins = nc.scalar.activation(h2[:, m, :], b_a[:, P * m:P * m + P], ACT.Relu, bias=col("b2", m))
                    ins.then_inc(h2_ready, 1)
                if cur and not prev:
                    if k == 0:
                        first_layer_dense([2, 3])
                    if k == 2:
                        pair_rows_scale(range(SQ))
                    if k == 3:
                        pair_rows_centre(range(SQ))

            x_std()
            first_layer_dense([0, 1])
            x_columns()
            walk(act, slot)

        @block.vector
        def _(dve):
            step = [0]

            def done(ins):
                step[0] += 1
                ins.then_inc(set_up, 1)
                dve.wait_ge(set_up, step[0])

            def ready(ins, s):
                ins.then_inc(s, 1)
                dve.wait_ge(s, 1)

            v = nc.vector
            dve.wait_ge(loaded["cols"], count["cols"])
            done(v.tensor_reduce(mean[:, 0:1], of("wsT"), AX.X, ALU.add))
            done(v.tensor_scalar(mean[:, 1:2], mean[:, 0:1], -1.0 / E, None, ALU.mult))
            ready(v.tensor_scalar(wsc[:], of("wsT"), mean[:, 1:2], None, ALU.add), wsc_ready)
            dve.wait_ge(loaded["wdT"], count["wdT"])
            done(v.tensor_reduce(mean[:, 2:4], wdT[:], AX.X, ALU.add))
            done(v.tensor_scalar(mean[:, 4:6], mean[:, 2:4], -1.0 / E, None, ALU.mult))
            for i in range(DK):
                ins = v.tensor_scalar(wdc[:, i, :], wdT[:, i, :], mean[:, 4 + i:5 + i], None, ALU.add)
            ready(ins, wdc_ready)

            dve.wait_ge(square_done, 1)
            ready(v.scalar_tensor_tensor(out=form[:], in0=b_t[:, 0, :], scalar=1.0 / E, in1=of("blk"), op0=ALU.mult, op1=ALU.mult), form_ready)
            dve.wait_ge(loaded["late_cols"], count["late_cols"])
            wrow = of("wrow").rearrange("p (c q) -> p c q", q=PROJ)
            done(v.tensor_reduce(nmean[:], wrow, AX.X, ALU.add))
            done(v.tensor_scalar(nmean[:], nmean[:], -1.0 / PROJ, None, ALU.mult))
            done(v.tensor_tensor(wcen[:], wrow, nmean[:].unsqueeze(2).broadcast_to([P, CHUNKS, PROJ]), ALU.add))
            for unit in PIECES:
                for c, lo, hi, off in unit:
                    nb = hi - lo + 1
                    ins = v.tensor_tensor(wbd[:, off:off + nb, :], wcen[:, c:c + 1, :].broadcast_to([P, nb, PROJ]),
                                          cols[:, COL["own"][0] + off:COL["own"][0] + off + nb].unsqueeze(2).broadcast_to([P, nb, PROJ]), ALU.mult)
            ready(ins, wbd_ready)

            def projection_weights():
                dve.wait_ge(tiles_set, 1)
                gsr = COL["gsr"]
                for h in range(2):
                    p = slice(64 * h, 64 * h + 64)
                    ins = v.tensor_tensor(ypad[p, h, :], wsc[p, :], cols[p, gsr[0]:gsr[1]], ALU.mult)
                ready(ins, ypad_ready)
                dve.wait_ge(loaded["bcols"], count["bcols"])
                v.tensor_copy(whole[:, 0:E], bof("bs")).then_inc(bs_placed, 1)
                wsum = whole[:, E:E + PROJ]
                done(v.tensor_reduce(wsum, bof("wsi").rearrange("p (q n) -> p q n", n=NT), AX.X, ALU.add))
                done(v.tensor_reduce(bmean[:, 0:1], wsum, AX.X, ALU.add))
                done(v.tensor_scalar(bmean[:, 1:2], bmean[:, 0:1], -1.0 / PROJ, None, ALU.mult))
                done(v.tensor_scalar(wsum, wsum, bmean[:, 1:2], None, ALU.add))
                dve.wait_ge(bs_placed, 1)
                done(v.tensor_copy(split[:, 0, :], whole[:]))
                done(v.tensor_tensor(rest[:, 0, :], whole[:], split[:, 0, :], ALU.subtract))
                done(v.tensor_copy(split[:, 1, :], rest[:, 0, :]))
                done(v.tensor_tensor(rest[:, 1, :], rest[:, 0, :], split[:, 1, :], ALU.subtract))
                done(v.tensor_copy(split[:, 2, :], rest[:, 1, :]))
                both = ((slice(0, E), "pick_bs", bias_l[0:R9, :]), (slice(E, E + PROJ), "pick_ws", picked[:]))
                for w, pick, dst in both:
                    ins = v.tensor_scalar(dst, split[:, 0, w], bof(pick)[:, 0:1], None, ALU.mult)
                done(ins)
                for j in (1, 2):
                    for w, pick, dst in both:
                        ins = v.scalar_tensor_tensor(out=dst, in0=split[:, j, w], scalar=bof(pick)[:, j:j + 1], in1=dst,
                                                     op0=ALU.mult, op1=ALU.add)
                    done(ins)
                ready(v.tensor_copy(bias_r[0:R9], picked[:].unsqueeze(1).broadcast_to([R9, UB, PROJ])), bias_ready)

            def x_scale():
                dve.wait_ge(xstd_ready, 1)
                done(v.reciprocal(xinv[:], xstd[:]))
                v.tensor_tensor(xn[:], b_f[:], xinv[:].unsqueeze(2).broadcast_to([P, GROUPS, E]), ALU.mult).then_inc(xn_ready, 1)

            def x_rows():
                dve.wait_ge(xsum_done, 1)
                ready(v.tensor_scalar(xone[64:96, :], b_a[64:96, :], col("one_row", 0, 64, 96), None, ALU.add), xone_ready)

            def sum_coefficients():
                ready(v.tensor_tensor(gg[:], of("gcol"), of("grow"), ALU.mult), gg_ready)
                dve.wait_ge(loaded["ce"], count["ce"])
                v.tensor_tensor(cg[:, 0, :], of("gI"), of("hJ"), ALU.mult)
                v.tensor_tensor(cg[:, 1, :], of("gJ"), of("hI"), ALU.mult)
                done(v.tensor_tensor(cg[:, 2, :], of("hI"), of("hJ"), ALU.mult))
                for c in range(PCH):
                    ins = v.tensor_scalar(cm[:, c, :], ce[:, 0, c, :], cg[:, 0, c:c + 1], None, ALU.mult)
                done(ins)
                for j in (1, 2):
                    for c in range(PCH):
                        ins = v.scalar_tensor_tensor(out=cm[:, c, :], in0=ce[:, j, c, :], scalar=cg[:, j, c:c + 1], in1=cm[:, c, :],
                                                     op0=ALU.mult, op1=ALU.add)
                    if j == 1:
                        done(ins)
                ready(ins, cm_ready)

            def pair_means():
                dve.wait_ge(wf_scaled, SQ)
                v.tensor_scalar(fmean[:, 0:SQ], fsum[:, 0:SQ], -1.0 / MAXD, None, ALU.mult).then_inc(fmean_ready, 1)

            def last_pair_rows():
                r, L = slice(0, SUMS), slice(WS - 1, WS)
                dve.wait_ge(sum_rows_done, 1)
                done(v.scalar_tensor_tensor(out=wf[r, WS - 1, :], in0=wf[r, WS - 1, :], scalar=gg[r, L], in1=bf[r], op0=ALU.mult, op1=ALU.add))
                done(v.tensor_reduce(fsum[:, L], wf[:, WS - 1, :], AX.X, ALU.add))
                done(v.tensor_scalar(fmean[:, L], fsum[:, L], -1.0 / MAXD, None, ALU.mult))
                v.tensor_scalar(wf[:, WS - 1, :], wf[:, WS - 1, :], fmean[:, L], None, ALU.add).then_inc(wf_ready, 1)

            def slot(s, k, cur, prev):
                ms, mk, m_on = earlier(s, k, 1, cur, prev)
                gs_, gk, g_on = earlier(s, k, 2, cur, prev)
                if prev and k == 2:
                    dve.wait_ge(zt_ready, 2 * UNITS * s)
                    dve.sem_inc(zt_seen, 1)
                    v.stream_shuffle(zt[:, SQ:2 * SQ, :], zt[:, SQ:2 * SQ, :], [16 + i % 16 for i in range(32)]).then_inc(zt_moved, 1)
                    dve.wait_ge(zt_moved, s)
                    dve.sem_inc(move_seen, 1)
                    v.copy_predicated(zt[:, 0:SQ, :], of("moved").bitcast(U32).unsqueeze(2).broadcast_to([P, SQ, P]),
                                      zt[:, SQ:2 * SQ, :]).then_inc(zt_packed, 1)
                if cur and not prev and k == 3:
                    pair_means()
                if cur:
                    c0, n = UNIT_CHUNKS[k][0], len(UNIT_CHUNKS[k])
                    U = upto(s, k)
                    src = emb[:, c0:c0 + n]
                    dve.wait_ge(form_done, U)
                    v.tensor_tensor(prod[:, 0:n, :], b_t[:, 0:n, :], src.rearrange("p c h d -> p c (h d)"), ALU.mult).then_inc(prod_ready, 1)
                    dve.wait_ge(prod_ready, U)
                    v.tensor_reduce(var1[:, 0:2 * n], prod[:, 0:n, :].rearrange("p c (h d) -> p (c h) d", h=2), AX.X, ALU.add).then_inc(sum1_ready, 1)
                    dve.wait_ge(sum1_ready, U)
                    v.tensor_scalar(var1[:, 0:2 * n], var1[:, 0:2 * n], 0.0, EPS, ALU.max, ALU.add).then_inc(var1_ready, 1)
                    dve.wait_ge(std1_ready, U)
                    v.reciprocal(inv1[:, 0:2 * n], std1[:, 0:2 * n]).then_inc(inv1_ready, 1)
                    dve.wait_ge(inv1_ready, U)
                    v.tensor_tensor(embr[:, c0:c0 + n].rearrange("p c h d -> p (c h) d"), src.rearrange("p c h d -> p (c h) d"),
                                    inv1[:, 0:2 * n].unsqueeze(2).broadcast_to([P, 2 * n, D]), ALU.mult).then_inc(embr_ready, 1)
                if prev and k == 3:
                    at = slice(P * (s - 1), P * s) if isinstance(s, int) else bass.ds(P * (s - 1), P)
                    for m in (0, 2):
                        dve.wait_ge(h1_done, 2 * s - 1 + m // 2)
                        v.tensor_tensor(h1s[:, m:m + 2, :], h1_banks[m // 2][:, m:m + 2, :], dd[:, m:m + 2, at], ALU.add).then_inc(h1_summed, 1)
                if m_on:
                    if not prev and k == 1:
                        dve.wait_ge(xt_ready, 1)
                    for h in range(2):
                        N = 2 * upto(ms, mk) - 1 + h
                        dve.wait_ge(sq_ready, N)
                        v.tensor_reduce(var2[h][:], sq[h][:].rearrange("p (b q) -> p b q", q=PROJ), AX.X, ALU.add).then_inc(var2_ready, 1)
                    for h in range(2):
                        N = 2 * upto(ms, mk) - 1 + h
                        uu = u[mk % 2][h]
                        dve.wait_ge(std2_ready, N)
                        v.reciprocal(inv2[h][:], std2[h][:]).then_inc(inv2_ready, 1)
                        b0 = P * ms + HALF * h + UB * mk
                        at = slice(b0, b0 + UB) if isinstance(ms, int) else bass.ds(b0, UB)
                        v.tensor_copy(uu[:, :, PROJ], xt[:, at]).then_inc(u_ready, 1)
                        dve.wait_ge(inv2_ready, N)
                        v.tensor_tensor(uu[:, :, 0:PROJ], b_y[h][:].rearrange("p (b q) -> p b q", q=PROJ),
                                        inv2[h][:].unsqueeze(2).broadcast_to([P, UB, PROJ]), ALU.mult).then_inc(u_ready, 1)
                if prev and k == 2:
                    dve.wait_ge(stdz_ready, s)
                    v.reciprocal(invz[:], stdz[:]).then_inc(invz_ready, 1)
                    dve.wait_ge(invz_ready, s)
                    v.tensor_scalar(zn[:], bf[:, 0:KEEP], invz[:], None, ALU.mult).then_inc(zn_ready, 1)
                if prev and k == 3:
                    dve.wait_ge(out_done, s)
                    at = slice(P * (s - 1), P * s) if isinstance(s, int) else bass.ds(P * (s - 1), P)
                    v.tensor_copy(yrow[0:1, at], b_f[0:1, 0, :]).then_inc(yrow_ready, 1)
                if cur and not prev:
                    if k == 0:
                        x_rows()
                    if k == 1:
                        sum_coefficients()
                    if k == 3:
                        last_pair_rows()

            x_scale()
            projection_weights()
            walk(dve, slot)


def shape_constants():
    rows = [12500, 1000, 12500, 1000, 1000, 1000, 12500, 125000, 1250, 125000, 125000, 1250, 12500, 1250, 12500, 1000,
            1250, 1250, 1250, 12500, 1250, 1250, 1250, 12500, 12500, 1250]
    first = np.concatenate([[0], np.cumsum(rows)[:-1]]).astype(np.int32)
    f = np.arange(CHUNKS * P)
    row_b, row_n = (f // NT).reshape(CHUNKS, P), (f % NT).reshape(CHUNKS, P)
    return first, row_b, row_n


def lay_out(inputs):
    g = {k: np.asarray(v) for k, v in inputs.items()}
    first, row_b, row_n = shape_constants()
    a = {}
    a["table"] = np.concatenate([g[f"tbl_{i}"] for i in range(NT)], axis=0)
    ids = g["ids"].reshape(GROUPS, 2, HALF, NT)
    joined = ids[:, :, row_b, row_n].transpose(3, 0, 2, 1).reshape(P, -1)
    base = np.repeat(first[row_n].T[:, :, None], 2, axis=2).reshape(P, -1)
    a["ids"] = np.ascontiguousarray(np.concatenate([joined, np.zeros_like(base), base], axis=1))
    wsi = g["L0_rec_Wsi"]
    a["wdT"] = np.ascontiguousarray(g["L0_rec_Wd"].T.reshape(DK, P, E).transpose(1, 0, 2))
    a["denT"] = np.ascontiguousarray(g["r_dense_t"].T.reshape(DK, P, BATCH).transpose(1, 0, 2))
    wl, gsi, bsi = g["L0_rec_Wl"], g["L0_rec_gsi"], g["L0_rec_bsi"]
    ti, tj = np.tril_indices(PROJ + 1, k=-1)
    pair = {(int(i), int(j)): n for n, (i, j) in enumerate(zip(ti, tj))}
    wf = np.zeros((4, PROJ, WS, MAXD), np.float32)
    grow, gcol = np.ones((2, 4, PROJ, WS), np.float32)
    moved = np.zeros((4, PROJ, SQ), np.float32)
    M = PROJ // 2
    for c in range(M):
        s, r = c // 4, c % 4
        for p in range(PROJ):
            i, j = (M + c, M + p) if p < c else (p, c)
            moved[r, p, s] = p < c
            grow[r, p, s], gcol[r, p, s] = gsi[i], gsi[j]
            if i > j:
                wf[r, p, s] = wl[:, pair[i + 1, j + 1]]
    for p in range(PROJ):
        wf[0, p, WS - 1] = wl[:, pair[p + 1, 0]]
        grow[0, p, WS - 1] = gsi[p]
    a["wf"] = wf.reshape(P, WS, MAXD)
    wlT = np.zeros((PCH * P, MAXD), np.float32)
    wlT[:NPAIR] = wl.T
    a["wlT"] = np.ascontiguousarray(wlT.reshape(PCH, P, MAXD).transpose(1, 0, 2))
    ce = np.zeros((3, PCH * P, P), np.float32)
    n = np.arange(NPAIR)
    real = tj > 0
    ce[0, n[real], 32 + ti[real] - 1] = 1.0
    ce[1, n[real], 32 + tj[real] - 1] = 1.0
    ce[1, n[~real], 64] = 1.0
    ce[2, n[real], 65] = E
    a["ce"] = np.ascontiguousarray(ce.reshape(3, PCH, P, P).transpose(2, 0, 1, 3)[:, :, :, :SUMS])
    w1 = np.concatenate([g["W_top1"][:KEEP], g["W_top1"][MAXD:]], axis=0)
    w1 = w1.reshape(ZK + DK, P, F1).transpose(1, 0, 2)
    a["w1z"], a["w1d"] = np.ascontiguousarray(w1[:, :ZK]), np.ascontiguousarray(w1[:, ZK:])
    a["w2"] = np.ascontiguousarray(g["W_top2"].reshape(MT1, P, F2).transpose(1, 0, 2))

    cols = np.zeros((P, NCOL), np.float32)

    def put(name, values):
        cols[:, COL[name][0]:COL[name][1]] = values

    put("wsT", np.concatenate([g["L0_rec_Ws"].T] * 2, axis=0))
    put("ident", np.eye(P))
    put("blk", np.kron(np.eye(2), np.ones((D, D))))
    put("gsr", g["L0_rec_gs"])
    put("wrow", wsi.T[row_n].transpose(1, 0, 2).reshape(P, -1))
    own = np.zeros((P, AB), np.float32)
    for unit in PIECES:
        for c, lo, hi, off in unit:
            own[:, off:off + hi - lo + 1] = row_b[c][:, None] == np.arange(lo, hi + 1)
    put("own", own)
    put("gd", g["L0_rec_gd"].reshape(P, 1))
    put("bd", g["L0_rec_bd"].reshape(P, 1))
    put("gl", g["L0_rec_gl"][:KEEP].reshape(ZK, P).T)
    put("bl", g["L0_rec_bl"][:KEEP].reshape(ZK, P).T)
    put("b1", g["b_top1"].reshape(MT1, P).T)
    put("b2", g["b_top2"].reshape(MT2, P).T)
    put("w3", g["W_top3"].reshape(MT2, P).T)
    put("grow", grow.reshape(P, WS))
    put("gcol", gcol.reshape(P, WS))
    put("moved", moved.reshape(P, SQ))

    def pairs(values, x_value):
        full = np.zeros(PCH * P, np.float32)
        full[:NPAIR] = values
        full[:NPAIR][x_value[0]] = x_value[1]
        return full.reshape(PCH, P).T

    never = np.zeros(NPAIR, bool)
    put("gI", pairs(gsi[ti - 1], (never, 0.0)))
    put("hI", pairs(bsi[ti - 1], (never, 0.0)))
    put("gJ", pairs(gsi[np.maximum(tj, 1) - 1], (~real, 1.0)))
    put("hJ", pairs(bsi[np.maximum(tj, 1) - 1], (~real, 0.0)))
    put("eps", EPS)
    cols[65, COL["one_row"][0]] = 1.0
    a["cols"] = cols
    bcols = np.zeros((PARTS * PARTS, NBCOL), np.float32)
    bcols[:, BCOL["bs"][0]:BCOL["bs"][1]] = g["L0_rec_bs"]
    bcols[:, BCOL["wsi"][0]:BCOL["wsi"][1]] = wsi.reshape(-1)
    for i in range(PARTS):
        for j in range(PARTS):
            bcols[PARTS * i + j, BCOL["pick_bs"][0] + i] = 1.0
            bcols[PARTS * i + j, BCOL["pick_ws"][0] + j] = 1.0
    a["bcols"] = bcols
    return a


def kernel(**inputs):
    import concourse.bacc as _bacc
    from concourse.bass_utils import run_bass_kernel_spmd as _run

    arrays = lay_out(inputs)
    nc = _bacc.Bacc("TRN2", target_bir_lowering=False, num_devices=1)
    t = {n: nc.dram_tensor("in_" + n, v.shape, mybir.dt.from_np(v.dtype), kind="ExternalInput").ap() for n, v in arrays.items()}
    out = nc.dram_tensor("out", (BATCH, 1), F32, kind="ExternalOutput").ap()
    program(nc, t, out)
    r = _run(nc, [{"in_" + n: v for n, v in arrays.items()}], core_ids=[0])
    return r.results[0]["out"]
```

```python
from contextlib import ExitStack

import numpy as np
import concourse.bass as bass
from concourse import mybir

F32 = mybir.dt.float32
BF16 = mybir.dt.bfloat16
I32 = mybir.dt.int32
U32 = mybir.dt.uint32
ALU = mybir.AluOpType
ACT = mybir.ActivationFunctionType
AX = mybir.AxisListType

P = 128
BATCH, NT, D = 512, 26, 64
DENSE, E, PROJ = 256, 128, 32
MAXD, KEEP = 512, 384
F1, F2 = 512, 256
EPS = 1e-5

GROUPS = BATCH // P
HALF = P // 2
CHUNKS = HALF * NT // P
UNITS = 4
UB = HALF // UNITS
UNIT_CHUNKS = [range(0, 4), range(4, 7), range(7, 10), range(10, 13)]
COLS = PROJ + 2
SQ = PROJ // 8
SLOTS = PROJ // 4 + 1
LAST = SLOTS - 1
PAIR_SLOTS = [*range(SQ), LAST]
WS = len(PAIR_SLOTS)
SUMS = PROJ + COLS
NPAIR = (PROJ + 1) * PROJ // 2
PCH = 5
ZK, DK = KEEP // P, DENSE // P
MT1, MT2 = F1 // P, F2 // P
OT = MAXD // P


def a_pieces():
    out, off = [], 0
    for k in range(UNITS):
        unit = []
        for c in range(CHUNKS):
            lo = max(UB * k, (P * c) // NT)
            hi = min(UB * k + UB - 1, (P * c + P - 1) // NT)
            if lo <= hi:
                unit.append((c, lo, hi, off))
                off += hi - lo + 1
        out.append(unit)
    return out, off


PIECES, AB = a_pieces()

COL = {}
NCOL = 0
for _name, _n in (("wsT", E), ("ident", P), ("blk", P), ("eps", 1), ("gsr", E), ("gd", 1), ("bd", 1), ("gl", ZK),
                  ("bl", ZK), ("b1", MT1), ("b2", MT2), ("w3", MT2), ("grow", WS), ("gcol", WS), ("gI", PCH),
                  ("gJ", PCH), ("hI", PCH), ("hJ", PCH), ("one_row", 1), ("moved", SQ), ("own", AB),
                  ("wrow", CHUNKS * PROJ)):
    COL[_name] = (NCOL, NCOL + _n)
    NCOL += _n


def program(nc, t, out):
    ctx = ExitStack()
    with ctx:
        def sb(name, shape, dt=F32):
            return ctx.enter_context(nc.sbuf_tensor(name, shape, dt))

        def bank(name, shape):
            return ctx.enter_context(nc.psum_tensor(name, shape, F32))

        def sem(name):
            return ctx.enter_context(nc.semaphore(name))

        ids = sb("ids", [P, (GROUPS + 2) * 2 * CHUNKS], I32)
        cols = sb("cols", [P, NCOL])
        brow = sb("brow", [P, E + PROJ * NT])
        wdT = sb("wdT", [P, DK, E])
        denT = sb("denT", [P, DK, BATCH])
        w1d = sb("w1d", [P, DK, F1])
        w1z = sb("w1z", [P, ZK, F1])
        wf = sb("wf", [P, WS, MAXD])
        wlT = sb("wlT", [P, PCH, MAXD])
        ce = sb("ce", [P, 3, PCH, SUMS])
        w2 = sb("w2", [P, MT1, F2])
        loads = dict(ids=ids, cols=cols, late_cols=cols, wdT=wdT, denT=denT, w1d=w1d, w1z=w1z, wf=wf, wlT=wlT, ce=ce, w2=w2)
        early = COL["gsr"][0]
        first_loads = [("ids", [slice(None)]), ("cols", [slice(0, early)]), ("wdT", [slice(None)]), ("denT", [0, 1]),
                       ("late_cols", [slice(early, NCOL)]), ("w1d", [0, 1])]
        later_loads = [("ce", range(3)), ("wlT", range(PCH)), ("wf", range(WS)), ("w1z", range(ZK)),
                       ("w2", [slice(0, 2), slice(2, 4)])]
        BIAS_ROW = (HALF, 0)
        count = {name: 16 * len(parts) for name, parts in first_loads + later_loads}

        def of(name):
            return cols[:, COL[name][0]:COL[name][1]]

        def col(name, i=0, p0=0, p1=P):
            return cols[p0:p1, COL[name][0] + i:COL[name][0] + i + 1]

        ident = of("ident")
        base = ids[:, (GROUPS + 1) * 2 * CHUNKS:(GROUPS + 2) * 2 * CHUNKS]

        idx = sb("idx", [P, 2, 2 * CHUNKS], I32)
        mean = sb("mean", [P, 8])
        wsc = sb("wsc", [P, E])
        wse = sb("wse", [P, 2 * D])
        form = sb("form", [P, P])
        ypad = sb("ypad", [P, 2, E])
        nmean = sb("nmean", [P, CHUNKS])
        wcen = sb("wcen", [P, CHUNKS, PROJ])
        wbd = sb("wbd", [P, AB, PROJ])
        wdc = sb("wdc", [P, DK, E])
        jcol = sb("jcol", [P, PROJ])
        wsum = sb("wsum", [P, PROJ])
        wmean = sb("wmean", [P, 2])
        zeros = sb("zeros", [P, E + 512], BF16)
        xsq = sb("xsq", [P, GROUPS, E])
        xvar = sb("xvar", [P, GROUPS])
        xstd = sb("xstd", [P, GROUPS])
        xinv = sb("xinv", [P, GROUPS])
        xn = sb("xn", [P, GROUPS, E])
        xt = sb("xt", [P, BATCH])
        xone = sb("xone", [P, BATCH])
        dd = sb("dd", [P, MT1, BATCH])
        cm = sb("cm", [P, PCH, SUMS])
        cg = sb("cg", [P, 3, PCH])
        term = sb("term", [P, 2, PCH, SUMS - 1])
        gg = sb("gg", [P, WS])
        fsum = sb("fsum", [P, WS])
        fmean = sb("fmean", [P, WS])

        emb = sb("emb", [P, CHUNKS, 2, D])
        embT = sb("embT", [P, 4, P])
        prod = sb("prod", [P, 4, P])
        var1 = sb("var1", [P, 8])
        std1 = sb("std1", [P, 8])
        inv1 = sb("inv1", [P, 8])
        embr = sb("embr", [P, CHUNKS, 2, D])
        aT = sb("aT", [P, 2, UB * PROJ])
        sq = [sb(f"sq{h}", [P, UB * PROJ]) for h in range(2)]
        var2 = [sb(f"var2{h}", [P, UB]) for h in range(2)]
        std2 = [sb(f"std2{h}", [P, UB]) for h in range(2)]
        inv2 = [sb(f"inv2{h}", [P, UB]) for h in range(2)]
        u = [[sb(f"u{k}{h}", [P, UB, COLS]) for h in range(2)] for k in range(2)]
        zt = sb("zt", [P, SLOTS, P])
        zsq = sb("zsq", [P, MAXD])
        varz = sb("varz", [P, 1])
        stdz = sb("stdz", [P, 1])
        invz = sb("invz", [P, 1])
        zn = sb("zn", [P, KEEP])
        zT = sb("zT", [P, ZK, P])
        h1s = sb("h1s", [P, MT1, P])
        h1 = sb("h1", [P, MT1, P])
        h2 = sb("h2", [P, MT2, P])
        yrow = sb("yrow", [1, BATCH])
        first_root = sb("first_root", [P, 1])

        b_tr = bank("b_tr", [P, 4, P])
        b_t = bank("b_t", [P, 4, P])
        b_a = bank("b_a", [P, 512])
        b_y = [bank(f"b_y{h}", [P, UB * PROJ]) for h in range(2)]
        b_z = bank("b_z", [P, 2, 512])
        b_f = bank("b_f", [P, OT, P])
        dd_banks = [b_y[0][:], b_y[1][:], b_z[:, 0, :], b_z[:, 1, :]]
        z_banks = [b_f, b_f, b_tr]
        h1_banks = [b_tr, b_f]
        bf = b_f[:].rearrange("p a b -> p (a b)")
        h2_banks = [b_a[:], b_t[:, 0, :]]

        loaded = {n: sem(f"loaded_{n}") for n in count}
        loaded_brow = sem("loaded_brow")
        gathered = [sem(f"gathered_{c}") for c in range(CHUNKS)]
        idx_ready = sem("idx_ready")
        chunk_free = sem("chunk_free")
        set_up = sem("set_up")
        wsc_ready = sem("wsc_ready")
        wsc_turned = sem("wsc_turned")
        wse_ready = sem("wse_ready")
        square_done = sem("square_done")
        form_ready = sem("form_ready")
        wdc_ready = sem("wdc_ready")
        dense_done = sem("dense_done")
        xvar_ready = sem("xvar_ready")
        xstd_ready = sem("xstd_ready")
        xn_ready = sem("xn_ready")
        x_turned = sem("x_turned")
        xt_ready = sem("xt_ready")
        tiles_cleared = sem("tiles_cleared")
        tiles_set = sem("tiles_set")
        xsum_done = sem("xsum_done")
        xone_ready = sem("xone_ready")
        wbd_ready = sem("wbd_ready")
        cm_ready = sem("cm_ready")
        bias_ready = sem("bias_ready")
        sum_rows_done = sem("sum_rows_done")
        wf_ready = sem("wf_ready")
        fmean_ready = sem("fmean_ready")
        gg_ready = sem("gg_ready")
        dd_done = sem("dd_done")
        dd_ready = sem("dd_ready")
        emb_turned = sem("emb_turned")
        embT_ready = sem("embT_ready")
        form_done = sem("form_done")
        prod_ready = sem("prod_ready")
        sum1_ready = sem("sum1_ready")
        var1_ready = sem("var1_ready")
        std1_ready = sem("std1_ready")
        inv1_ready = sem("inv1_ready")
        embr_ready = sem("embr_ready")
        a_done = sem("a_done")
        aT_ready = sem("aT_ready")
        y_done = sem("y_done")
        sq_ready = sem("sq_ready")
        var2_ready = sem("var2_ready")
        std2_ready = sem("std2_ready")
        inv2_ready = sem("inv2_ready")
        u_ready = sem("u_ready")
        gram_done = sem("gram_done")
        zt_ready = sem("zt_ready")
        zt_x_ready = sem("zt_x_ready")
        pairs_done = sem("pairs_done")
        zt_seen = sem("zt_seen")
        zt_moved = sem("zt_moved")
        move_seen = sem("move_seen")
        zt_part_packed = sem("zt_part_packed")
        zt_packed = sem("zt_packed")
        varz_ready = sem("varz_ready")
        stdz_ready = sem("stdz_ready")
        invz_ready = sem("invz_ready")
        zn_ready = sem("zn_ready")
        z_turned = sem("z_turned")
        zT_by_act = sem("zT_by_act")
        zT_by_dve = sem("zT_by_dve")
        h1_summed = sem("h1_summed")
        h1_done = sem("h1_done")
        h1_ready = sem("h1_ready")
        h2_done = sem("h2_done")
        h2_ready = sem("h2_ready")
        out_done = sem("out_done")
        yrow_ready = sem("yrow_ready")
        stored = sem("stored")
        block = ctx.enter_context(nc.Block())

        def wait(eng, s, value):
            if not isinstance(value, int) or value > 0:
                eng.wait_ge(s, value)

        def upto(s, k):
            return UNITS * s + k + 1

        def walk(eng, slot):
            for k in range(UNITS):
                slot(0, k, True, False)
            with eng.Fori(1, GROUPS - 1) as s:
                for k in range(UNITS):
                    slot(s, k, True, True)
            for k in range(UNITS):
                slot(GROUPS - 1, k, True, True)
            for k in range(UNITS):
                slot(GROUPS, k, False, True)

        def mlp_here(s, k, cur, prev):
            return prev and k == 3 and not (cur and isinstance(s, int) and s == GROUPS - 1)

        def earlier(s, k, back, cur, prev):
            return (s, k - back, cur) if k >= back else (s - 1, k - back + UNITS, prev)

        def out_row(s):
            return (b_t if isinstance(s, int) and s == GROUPS - 1 else b_f)[0:1, 0, :]

        def gram_copy(k, h, r):
            q = 32 * (2 * (k % 2) + h)
            n = SLOTS if r < COLS - PROJ else SLOTS - 1
            b0 = HALF * h + UB * k
            src = b_z[q:q + PROJ, :, 0:8 * COLS].rearrange("p t (g c) -> p t g c", c=COLS)[:, :, :, r:r + 4 * (n - 1) + 1:4]
            dst = zt[32 * r:32 * r + PROJ, 0:n, b0:b0 + UB].rearrange("p s (t g) -> p t g s", t=2)
            return dst, src

        @block.sync
        def _(sp):
            for n, parts in first_loads:
                for part in parts:
                    src = t["cols" if n == "late_cols" else n]
                    sp.dma_start(loads[n][:, part], src[:, part]).then_inc(loaded[n], 16)
            for row in BIAS_ROW:
                sp.dma_start(brow[row:row + 1, :], t["brow"]).then_inc(loaded_brow, 16)
            later = [(n, part) for n, parts in later_loads for part in parts]
            for i, (n, part) in enumerate(later):
                if i % 2 == 0:
                    sp.wait_ge(gathered[i // 2], 32)
                sp.dma_start(loads[n][:, part], t[n][:, part]).then_inc(loaded[n], 16)
            sp.wait_ge(yrow_ready, GROUPS + 1)
            sp.dma_start(out.rearrange("b o -> o b"), yrow[0:1, :]).then_inc(stored, 16)
            sp.wait_ge(stored, 16)

        @block.gpsimd
        def _(pool):
            SPLIT = 7
            NI = 2 * CHUNKS
            for tile in (ypad[:], aT[:], zeros[:], jcol[:], zt[:, LAST, :]):
                nc.gpsimd.memset(tile, 0.0).then_inc(tiles_cleared, 1)
            pool.wait_ge(tiles_cleared, 5)
            nc.gpsimd.memset(jcol[:, 0:1], 1.0).then_inc(tiles_set, 1)
            nc.gpsimd.memset(yrow[:], 0.0).then_inc(yrow_ready, 1)
            for k in range(2):
                for h in range(2):
                    nc.gpsimd.memset(u[k][h][:, :, PROJ + 1], 1.0).then_inc(tiles_set, 1)
            pool.wait_ge(loaded["ids"], count["ids"])

            def index(s, late, count):
                lo, hi = (0, 2 * SPLIT) if not late else (2 * SPLIT, NI)
                at = bass.ds(s * NI + lo, hi - lo) if not isinstance(s, int) else slice(s * NI + lo, s * NI + hi)
                nc.gpsimd.tensor_tensor(idx[:, late, lo:hi], ids[:, at], base[:, lo:hi], ALU.add).then_inc(idx_ready, 1)
                pool.wait_ge(idx_ready, count)

            def gather(s, chunks, late):
                for c in chunks:
                    k = next(k for k in range(UNITS) if c in UNIT_CHUNKS[k])
                    if not isinstance(s, int):
                        pool.wait_ge(embr_ready, upto(s - 1, k))
                        pool.sem_inc(chunk_free, 1)
                    for h in range(2):
                        nc.gpsimd.indirect_dma_start(
                            emb[:, c, h, :], None, t["table"],
                            bass.IndirectOffsetOnAxis(ap=idx[:, late, 2 * c + h:2 * c + h + 1].bitcast(U32), axis=0),
                        ).then_inc(gathered[c], 16)

            index(0, 0, 1)
            index(0, 1, 2)
            gather(0, range(SPLIT), 0)
            gather(0, range(SPLIT, CHUNKS), 1)
            for c in range(SPLIT):
                pool.wait_ge(gathered[c], 32)
            index(1, 0, 3)
            with pool.Fori(1, GROUPS) as s:
                gather(s, range(SPLIT), 0)
                for c in range(SPLIT, CHUNKS):
                    pool.wait_ge(gathered[c], 32 * s)
                index(s, 1, 2 * s + 2)
                gather(s, range(SPLIT, CHUNKS), 1)
                for c in range(SPLIT):
                    pool.wait_ge(gathered[c], 32 * s + 32)
                index(s + 1, 0, 2 * s + 3)

        @block.tensor
        def _(pe):
            pe.wait_ge(wsc_ready, 1)
            nc.tensor.transpose(b_tr[:, 0, :], wsc[:], ident).then_inc(wsc_turned, 1)
            pe.wait_ge(wse_ready, 1)
            nc.tensor.matmul(b_t[:, 0, :], wse[:], wse[:], start=True, stop=True).then_inc(square_done, 1)
            pe.wait_ge(form_ready, 1)

            def dense_product():
                pe.wait_ge(wdc_ready, 1)
                pe.wait_ge(loaded["denT"], count["denT"])
                for g in range(GROUPS):
                    for i in range(DK):
                        mm = nc.tensor.matmul(b_f[:, g, :], denT[:, i, P * g:P * g + P], wdc[:, i, :], start=(i == 0), stop=(i == DK - 1))
                mm.then_inc(dense_done, 1)

            def first_layer_dense(blocks):
                pe.wait_ge(loaded["w1d"], count["w1d"])
                for m in blocks:
                    for i in range(DK):
                        mm = nc.tensor.matmul(dd_banks[m], w1d[:, i, P * m:P * m + P], denT[:, i, :], start=(i == 0), stop=(i == DK - 1))
                    mm.then_inc(dd_done, 1)

            def turn_x():
                pe.wait_ge(xn_ready, 1)
                for g in range(GROUPS):
                    mm = nc.tensor.transpose(b_f[:, g, :], xn[:, g, :], ident)
                mm.then_inc(x_turned, 1)

            def sum_x():
                pe.wait_ge(tiles_set, 1)
                pe.wait_ge(xt_ready, 1)
                nc.tensor.matmul(b_a[64:96, :], jcol[:], xt[:], start=True, stop=True).then_inc(xsum_done, 1)

            def sum_rows():
                pe.wait_ge(cm_ready, 2)
                pe.wait_ge(loaded["wlT"], count["wlT"])
                for c in range(PCH):
                    mm = nc.tensor.matmul(bf[0:SUMS], cm[:, c, :], wlT[:, c, :], start=(c == 0), stop=(c == PCH - 1))
                mm.then_inc(sum_rows_done, 1)

            def keep_warm(n, bank_):
                for i in range(n):
                    nc.tensor.matmul(bank_, zeros[:, 0:E], zeros[:, E:], start=True, stop=True)

            def first_layer(s):
                pe.wait_ge(loaded["w1z"], count["w1z"])
                pe.wait_ge(zT_by_act, 2 * s)
                pe.wait_ge(zT_by_dve, s)
                for m in range(MT1):
                    for i in range(ZK):
                        mm = nc.tensor.matmul(h1_banks[m // 2][:, m, :], w1z[:, i, P * m:P * m + P], zT[:, i, :], start=(i == 0), stop=(i == ZK - 1))
                    if m % 2 == 1:
                        mm.then_inc(h1_done, 1)

            def second_layer(s):
                pe.wait_ge(loaded["w2"], count["w2"])
                pe.wait_ge(h1_ready, 2 * s)
                if isinstance(s, int) and s == GROUPS:
                    pe.wait_ge(yrow_ready, s)
                for m in range(MT2):
                    for i in range(MT1):
                        mm = nc.tensor.matmul(h2_banks[m][:, 0:P], w2[:, i, P * m:P * m + P], h1[:, i, :], start=(i == 0), stop=(i == MT1 - 1))
                    mm.then_inc(h2_done, 1)

            def last_layer(s):
                pe.wait_ge(h2_ready, 2 * s)
                for i in range(MT2):
                    mm = nc.tensor.matmul(out_row(s), col("w3", i), h2[:, i, :], start=(i == 0), stop=(i == MT2 - 1))
                mm.then_inc(out_done, 1)

            def gram(s, k, h, prev):
                U = upto(s, k)
                pe.wait_ge(u_ready, 4 * U - 2 + 2 * h)
                if not prev and k == 0 and h == 0:
                    pe.wait_ge(tiles_set, 5)
                    pe.wait_ge(dd_ready, MT1)
                wait(pe, zt_ready, 2 * U - 5 + h)
                q = 32 * (2 * (k % 2) + h)
                uu = u[k % 2][h]
                for g in range(UB):
                    mm = nc.tensor.matmul(b_z[q:q + PROJ, g // 8, COLS * (g % 8):COLS * (g % 8) + COLS],
                                          uu[:, g, 0:PROJ], uu[:, g, :], start=True, stop=True)
                mm.then_inc(gram_done, 1)

            def slot(s, k, cur, prev):
                ms, mk, m_on = earlier(s, k, 1, cur, prev)
                gs_, gk, g_on = earlier(s, k, 2, cur, prev)
                if cur:
                    for i, c in enumerate(UNIT_CHUNKS[k]):
                        pe.wait_ge(gathered[c], 32 * (s + 1))
                        mm = nc.tensor.transpose(b_tr[:, i, :], emb[:, c].rearrange("p h d -> p (h d)"), ident)
                    mm.then_inc(emb_turned, 1)
                if m_on:
                    if not prev and k == 1:
                        pe.wait_ge(wbd_ready, 1)
                        pe.wait_ge(xone_ready, 1)
                    pe.wait_ge(embr_ready, upto(ms, mk))
                    for i, (c, lo, hi, off) in enumerate(PIECES[mk]):
                        nb = hi - lo + 1
                        o = (lo - UB * mk) * PROJ
                        mm = nc.tensor.matmul(b_a[:, o:o + nb * PROJ], embr[:, c].rearrange("p h d -> p (h d)"),
                                              wbd[:, off:off + nb, :].rearrange("p b q -> p (b q)"),
                                              start=(i == 0), stop=(i == len(PIECES[mk]) - 1), skip_group_check=True)
                    mm.then_inc(a_done, 1)
                if prev and k == 3:
                    pe.wait_ge(zn_ready, s)
                    if cur:
                        pe.wait_ge(embT_ready, upto(s, k))
                    for i in range(ZK):
                        mm = nc.tensor.transpose(z_banks[i][:, i, :], zn[:, P * i:P * i + P], ident)
                        if i > 0:
                            mm.then_inc(z_turned, 1)
                    if not cur:
                        last_layer(s - 1)
                if cur:
                    pe.wait_ge(embT_ready, upto(s, k))
                    wait(pe, prod_ready, upto(s, k) - 1)
                    for i, c in enumerate(UNIT_CHUNKS[k]):
                        mm = nc.tensor.matmul(b_t[:, i, :], embT[:, i, :], form[:], start=True, stop=True)
                    mm.then_inc(form_done, 1)
                if g_on:
                    gram(gs_, gk, 0, prev)
                if mlp_here(s, k, cur, prev):
                    first_layer(s)
                    if not cur:
                        keep_warm(5, b_z[:, 0, :])
                if m_on:
                    if not prev and k == 1:
                        pe.wait_ge(bias_ready, 1)
                        pe.wait_ge(tiles_set, 1)
                        pe.wait_ge(dd_ready, 2)
                    for h in range(2):
                        pe.wait_ge(aT_ready, 2 * upto(ms, mk) - 1 + h)
                        if prev or k > 1:
                            pe.wait_ge(u_ready, 4 * upto(ms, mk) - 6 + 2 * h)
                        nc.tensor.matmul(b_y[h][:], ypad[:, h, :], aT[:, h, :], start=True, stop=True).then_inc(y_done, 1)
                if prev and k == 2:
                    pe.wait_ge(zt_packed, s)
                    if not cur:
                        pe.wait_ge(zt_part_packed, 1)
                    pe.wait_ge(zt_x_ready, s)
                    if cur:
                        pe.wait_ge(yrow_ready, s)
                    else:
                        pe.wait_ge(h1_summed, 2 * s - 2)
                    pe.wait_ge(wf_ready, WS)
                    for i, slot_ in enumerate(PAIR_SLOTS):
                        mm = nc.tensor.matmul(bf, zt[:, slot_, :], wf[:, i, :], start=(i == 0), stop=(i == WS - 1))
                    mm.then_inc(pairs_done, 1)
                if mlp_here(s, k, cur, prev):
                    second_layer(s)
                if g_on:
                    gram(gs_, gk, 1, prev)
                if not cur and k == 0:
                    first_layer(s - 1)
                if not cur and k == 2:
                    second_layer(s - 1)
                if not cur and k < 2:
                    keep_warm((0, 8)[k], b_t[:].rearrange("p a b -> p (a b)"))
                if mlp_here(s, k, cur, prev):
                    last_layer(s)
                if cur and not prev:
                    if k == 0:
                        sum_x()
                        first_layer_dense([2, 3])
                    if k == 1:
                        sum_rows()

            dense_product()
            first_layer_dense([0, 1])
            turn_x()
            walk(pe, slot)

        @block.scalar
        def _(act):
            act.wait_ge(loaded["cols"], count["cols"])
            nc.scalar.activation(first_root[:], col("eps"), ACT.Sqrt)
            act.wait_ge(wsc_turned, 1)
            nc.scalar.copy(wse[:], b_tr[:, 0, :]).then_inc(wse_ready, 1)

            def x_std():
                act.wait_ge(dense_done, 1)
                for g in range(GROUPS):
                    nc.scalar.activation(xsq[:, g, :], b_f[:, g, :], ACT.Square, accum_out=xvar[:, g:g + 1]).then_inc(xvar_ready, 1)
                act.wait_ge(xvar_ready, GROUPS)
                nc.scalar.activation(xstd[:], xvar[:], ACT.Sqrt, scale=1.0 / E, bias=col("eps")).then_inc(xstd_ready, 1)

            def first_layer_dense(blocks):
                act.wait_ge(loaded["late_cols"], count["late_cols"])
                for m in blocks:
                    act.wait_ge(dd_done, m + 1)
                    nc.scalar.activation(dd[:, m, :], dd_banks[m], ACT.Identity, bias=col("b1", m)).then_inc(dd_ready, 1)

            def x_columns():
                act.wait_ge(x_turned, 1)
                nc.scalar.activation(xt[:], bf, ACT.Identity, scale=col("gd"), bias=col("bd")).then_inc(xt_ready, 1)

            def pair_rows():
                act.wait_ge(loaded["wf"], count["wf"])
                act.wait_ge(fmean_ready, 1)
                for i in range(SQ):
                    nc.scalar.activation(wf[:, i, :], wf[:, i, :], ACT.Identity, scale=gg[:, i:i + 1],
                                         bias=fmean[:, i:i + 1]).then_inc(wf_ready, 1)

            def copy_gram(s, k, h):
                act.wait_ge(gram_done, 2 * upto(s, k) - 1 + h)
                if k == 0 and h == 0 and (not isinstance(s, int) or s > 0):
                    act.wait_ge(pairs_done, s)
                for r in range(4):
                    ins = nc.scalar.copy(*gram_copy(k, h, r))
                ins.then_inc(zt_ready, 1)

            def second_root(s, k, h):
                act.wait_ge(var2_ready, 2 * upto(s, k) - 1 + h)
                nc.scalar.activation(std2[h][:], var2[h][:], ACT.Sqrt, scale=1.0 / PROJ, bias=col("eps")).then_inc(std2_ready, 1)

            def first_relu(s):
                for m in (0, 2):
                    act.wait_ge(h1_summed, 2 * s - 1 + m // 2)
                    nc.scalar.activation(h1[:, m:m + 2, :], h1s[:, m:m + 2, :], ACT.Relu).then_inc(h1_ready, 1)

            def second_relu(s):
                for m in range(MT2):
                    act.wait_ge(h2_done, 2 * s - 1 + m)
                    nc.scalar.activation(h2[:, m, :], h2_banks[m][:, 0:P], ACT.Relu, bias=col("b2", m)).then_inc(h2_ready, 1)

            def slot(s, k, cur, prev):
                ms, mk, m_on = earlier(s, k, 1, cur, prev)
                gs_, gk, g_on = earlier(s, k, 2, cur, prev)
                hs, hk, h_on = earlier(s, k, 3, cur, prev)
                if cur:
                    n = len(UNIT_CHUNKS[k])
                    act.wait_ge(emb_turned, upto(s, k))
                    nc.scalar.copy(embT[:, 0:n, :], b_tr[:, 0:n, :]).then_inc(embT_ready, 1)
                if g_on and k != 3 and (prev or k != 2):
                    second_root(gs_, gk, 1)
                if prev and k == 3:
                    act.wait_ge(z_turned, 2 * s - 1)
                    for i in range(ZK - 1):
                        nc.scalar.activation(zT[:, i, :], b_f[:, i, :], ACT.Identity, scale=col("gl", i), bias=col("bl", i)).then_inc(zT_by_act, 1)
                if m_on:
                    act.wait_ge(a_done, upto(ms, mk))
                    if not prev and k == 1:
                        act.wait_ge(tiles_set, 1)
                    for h in range(2):
                        p = slice(HALF * h, HALF * h + HALF)
                        nc.scalar.copy(aT[p, h, :], b_a[p, :]).then_inc(aT_ready, 1)
                if h_on and hk == 0:
                    copy_gram(hs, hk, 0)
                    at = slice(P * hs, P * hs + P) if isinstance(hs, int) else bass.ds(P * hs, P)
                    if not prev:
                        act.wait_ge(tiles_set, 1)
                        act.wait_ge(xone_ready, 1)
                    nc.scalar.copy(zt[64:96, LAST, :], xone[64:96, at]).then_inc(zt_x_ready, 1)
                if h_on:
                    copy_gram(hs, hk, 1)
                if not cur and k == 2:
                    first_relu(s - 1)
                if cur and not prev and k == 2:
                    pair_rows()
                if g_on and k in (0, 1):
                    copy_gram(gs_, gk, 0)
                if cur:
                    n = 2 * len(UNIT_CHUNKS[k])
                    act.wait_ge(var1_ready, upto(s, k))
                    nc.scalar.activation(std1[:, 0:n], var1[:, 0:n], ACT.Sqrt).then_inc(std1_ready, 1)
                if mlp_here(s, k, cur, prev):
                    first_relu(s)
                if m_on:
                    for h in range(2):
                        act.wait_ge(y_done, 2 * upto(ms, mk) - 1 + h)
                        nc.scalar.activation(sq[h][:], b_y[h][:], ACT.Square).then_inc(sq_ready, 1)
                    if g_on and k == 3:
                        copy_gram(gs_, gk, 0)
                    second_root(ms, mk, 0)
                    if k == 2 or k == 1 and not prev:
                        second_root(ms, mk, 1)
                if prev and k == 2:
                    act.wait_ge(pairs_done, s)
                    nc.scalar.activation(zsq[:], bf, ACT.Square, accum_out=varz[:]).then_inc(varz_ready, 1)
                    act.wait_ge(varz_ready, s)
                    nc.scalar.activation(stdz[:], varz[:], ACT.Sqrt, scale=1.0 / MAXD, bias=col("eps")).then_inc(stdz_ready, 1)
                if mlp_here(s, k, cur, prev) or not cur and k == 2:
                    second_relu(s if k == 3 else s - 1)
                if cur and not prev:
                    if k == 0:
                        first_layer_dense([2, 3])

            x_std()
            first_layer_dense([0, 1])
            x_columns()
            walk(act, slot)

        @block.vector
        def _(dve):
            step = [0]

            def done(ins):
                step[0] += 1
                ins.then_inc(set_up, 1)
                dve.wait_ge(set_up, step[0])

            def ready(ins, s):
                ins.then_inc(s, 1)
                dve.wait_ge(s, 1)

            v = nc.vector
            dve.wait_ge(loaded["cols"], count["cols"])
            done(v.tensor_reduce(mean[:, 0:1], of("wsT"), AX.X, ALU.add))
            done(v.tensor_scalar(mean[:, 1:2], mean[:, 0:1], -1.0 / E, None, ALU.mult))
            ready(v.tensor_scalar(wsc[:], of("wsT"), mean[:, 1:2], None, ALU.add), wsc_ready)
            dve.wait_ge(loaded["wdT"], count["wdT"])
            done(v.tensor_reduce(mean[:, 2:4], wdT[:], AX.X, ALU.add))
            done(v.tensor_scalar(mean[:, 4:6], mean[:, 2:4], -1.0 / E, None, ALU.mult))
            for i in range(DK):
                ins = v.tensor_scalar(wdc[:, i, :], wdT[:, i, :], mean[:, 4 + i:5 + i], None, ALU.add)
            ready(ins, wdc_ready)

            dve.wait_ge(square_done, 1)
            ready(v.scalar_tensor_tensor(out=form[:], in0=b_t[:, 0, :], scalar=1.0 / E, in1=of("blk"), op0=ALU.mult, op1=ALU.mult), form_ready)
            dve.wait_ge(loaded["late_cols"], count["late_cols"])
            wrow = of("wrow").rearrange("p (c q) -> p c q", q=PROJ)
            done(v.tensor_reduce(nmean[:], wrow, AX.X, ALU.add))
            done(v.tensor_scalar(nmean[:], nmean[:], -1.0 / PROJ, None, ALU.mult))
            done(v.tensor_tensor(wcen[:], wrow, nmean[:].unsqueeze(2).broadcast_to([P, CHUNKS, PROJ]), ALU.add))
            for unit in PIECES:
                for c, lo, hi, off in unit:
                    nb = hi - lo + 1
                    ins = v.tensor_tensor(wbd[:, off:off + nb, :], wcen[:, c:c + 1, :].broadcast_to([P, nb, PROJ]),
                                          cols[:, COL["own"][0] + off:COL["own"][0] + off + nb].unsqueeze(2).broadcast_to([P, nb, PROJ]), ALU.mult)
            ready(ins, wbd_ready)

            def projection_weights():
                dve.wait_ge(tiles_set, 1)
                gsr = COL["gsr"]
                for h in range(2):
                    p = slice(64 * h, 64 * h + 64)
                    ins = v.tensor_tensor(ypad[p, h, :], wsc[p, :], cols[p, gsr[0]:gsr[1]], ALU.mult)
                dve.wait_ge(loaded_brow, 32)
                rows = [slice(r, r + 1) for r in BIAS_ROW]
                for h, r in enumerate(rows):
                    v.tensor_copy(ypad[r, h, :], brow[r, 0:E])
                    ins = v.tensor_reduce(wsum[r, :], brow[r, E:].rearrange("p (q n) -> p q n", n=NT), AX.X, ALU.add)
                done(ins)
                for r in rows:
                    ins = v.tensor_reduce(wmean[r, 0:1], wsum[r, :], AX.X, ALU.add)
                done(ins)
                for r in rows:
                    ins = v.tensor_scalar(wmean[r, 1:2], wmean[r, 0:1], -1.0 / PROJ, None, ALU.mult)
                done(ins)
                for h, r in enumerate(rows):
                    ins = v.tensor_scalar(aT[r, h, :].rearrange("p (b q) -> p b q", q=PROJ), wsum[r, :].unsqueeze(1).broadcast_to([1, UB, PROJ]),
                                          wmean[r, 1:2], None, ALU.add)
                ready(ins, bias_ready)

            def x_scale():
                dve.wait_ge(xstd_ready, 1)
                done(v.reciprocal(xinv[:], xstd[:]))
                v.tensor_tensor(xn[:], b_f[:], xinv[:].unsqueeze(2).broadcast_to([P, GROUPS, E]), ALU.mult).then_inc(xn_ready, 1)

            def x_rows():
                dve.wait_ge(xsum_done, 1)
                ready(v.tensor_scalar(xone[64:96, :], b_a[64:96, :], col("one_row", 0, 64, 96), None, ALU.add), xone_ready)

            def sum_coefficients():
                ready(v.tensor_tensor(gg[:], of("gcol"), of("grow"), ALU.mult), gg_ready)
                dve.wait_ge(loaded["ce"], count["ce"])
                v.tensor_tensor(cg[:, 0, :], of("gI"), of("hJ"), ALU.mult)
                v.tensor_tensor(cg[:, 1, :], of("gJ"), of("hI"), ALU.mult)
                done(v.tensor_tensor(cg[:, 2, :], of("hI"), of("hJ"), ALU.mult))
                wide = [P, PCH, SUMS - 1]
                for j in range(2):
                    ins = v.tensor_tensor(term[:, j], ce[:, j, :, 0:SUMS - 1], cg[:, j, :].unsqueeze(2).broadcast_to(wide), ALU.mult)
                v.tensor_tensor(cm[:, :, SUMS - 1], ce[:, 2, :, SUMS - 1], cg[:, 2, :], ALU.mult).then_inc(cm_ready, 1)
                done(ins)
                v.tensor_tensor(cm[:, :, 0:SUMS - 1], term[:, 0], term[:, 1], ALU.add).then_inc(cm_ready, 1)

            def pair_means():
                dve.wait_ge(loaded["wf"], count["wf"])
                done(v.tensor_reduce(fsum[:, 0:SQ], wf[:, 0:SQ, :], AX.X, ALU.add))
                v.scalar_tensor_tensor(out=fmean[:, 0:SQ], in0=fsum[:, 0:SQ], scalar=-1.0 / MAXD, in1=gg[:, 0:SQ],
                                       op0=ALU.mult, op1=ALU.mult).then_inc(fmean_ready, 1)

            def last_pair_rows():
                r, L = slice(0, SUMS), slice(WS - 1, WS)
                dve.wait_ge(sum_rows_done, 1)
                done(v.scalar_tensor_tensor(out=wf[r, WS - 1, :], in0=wf[r, WS - 1, :], scalar=gg[r, L], in1=bf[r], op0=ALU.mult, op1=ALU.add))
                done(v.tensor_reduce(fsum[:, L], wf[:, WS - 1, :], AX.X, ALU.add))
                done(v.tensor_scalar(fmean[:, L], fsum[:, L], -1.0 / MAXD, None, ALU.mult))
                v.tensor_scalar(wf[:, WS - 1, :], wf[:, WS - 1, :], fmean[:, L], None, ALU.add).then_inc(wf_ready, 1)

            def first_layer_sum(s):
                at = slice(P * (s - 1), P * s) if isinstance(s, int) else bass.ds(P * (s - 1), P)
                for m in (0, 2):
                    dve.wait_ge(h1_done, 2 * s - 1 + m // 2)
                    v.tensor_tensor(h1s[:, m:m + 2, :], h1_banks[m // 2][:, m:m + 2, :], dd[:, m:m + 2, at], ALU.add).then_inc(h1_summed, 1)

            def keep_output(s):
                dve.wait_ge(out_done, s)
                at = slice(P * (s - 1), P * s) if isinstance(s, int) else bass.ds(P * (s - 1), P)
                v.tensor_copy(yrow[0:1, at], out_row(s)).then_inc(yrow_ready, 1)

            def pack(b0, b1, copied, moved, signal):
                halves = zt[:].rearrange("p c (h b) -> p c h b", h=2)
                first, last = halves[:, 0:SQ, :, b0:b1], halves[:, SQ:2 * SQ, :, b0:b1]
                dve.wait_ge(zt_ready, copied)
                dve.sem_inc(zt_seen, 1)
                v.stream_shuffle(last, last, [16 + i % 16 for i in range(32)]).then_inc(zt_moved, 1)
                dve.wait_ge(zt_moved, moved)
                dve.sem_inc(move_seen, 1)
                mask = of("moved").bitcast(U32).unsqueeze(2).unsqueeze(3).broadcast_to([P, SQ, 2, b1 - b0])
                v.copy_predicated(first, mask, last).then_inc(signal, 1)

            def slot(s, k, cur, prev):
                ms, mk, m_on = earlier(s, k, 1, cur, prev)
                gs_, gk, g_on = earlier(s, k, 2, cur, prev)
                if not cur and k == 1:
                    first_layer_sum(s - 1)
                    pack(0, UB * (UNITS - 1), 2 * UNITS * s - 2, s, zt_part_packed)
                if prev and k == 2:
                    if cur:
                        pack(0, HALF, 2 * UNITS * s, s, zt_packed)
                    else:
                        pack(UB * (UNITS - 1), HALF, 2 * UNITS * s, s + 1, zt_packed)
                if prev and k == 3:
                    i = ZK - 1
                    dve.wait_ge(z_turned, 2 * s)
                    v.tensor_scalar(zT[:, i, :], b_tr[:, i, :], col("gl", i), col("bl", i), ALU.mult, ALU.add).then_inc(zT_by_dve, 1)
                    if not cur:
                        keep_output(s - 1)
                if cur:
                    c0, n = UNIT_CHUNKS[k][0], len(UNIT_CHUNKS[k])
                    U = upto(s, k)
                    src = emb[:, c0:c0 + n]
                    dve.wait_ge(form_done, U)
                    v.tensor_tensor(prod[:, 0:n, :], b_t[:, 0:n, :], src.rearrange("p c h d -> p c (h d)"), ALU.mult).then_inc(prod_ready, 1)
                    dve.wait_ge(prod_ready, U)
                    v.tensor_reduce(var1[:, 0:2 * n], prod[:, 0:n, :].rearrange("p c (h d) -> p (c h) d", h=2), AX.X, ALU.add).then_inc(sum1_ready, 1)
                    dve.wait_ge(sum1_ready, U)
                    v.tensor_scalar(var1[:, 0:2 * n], var1[:, 0:2 * n], 0.0, EPS, ALU.max, ALU.add).then_inc(var1_ready, 1)
                    dve.wait_ge(std1_ready, U)
                    v.reciprocal(inv1[:, 0:2 * n], std1[:, 0:2 * n]).then_inc(inv1_ready, 1)
                    dve.wait_ge(inv1_ready, U)
                    v.tensor_tensor(embr[:, c0:c0 + n].rearrange("p c h d -> p (c h) d"), src.rearrange("p c h d -> p (c h) d"),
                                    inv1[:, 0:2 * n].unsqueeze(2).broadcast_to([P, 2 * n, D]), ALU.mult).then_inc(embr_ready, 1)
                if mlp_here(s, k, cur, prev):
                    first_layer_sum(s)
                if m_on:
                    if not prev and k == 1:
                        dve.wait_ge(xt_ready, 1)
                    for h in range(2):
                        N = 2 * upto(ms, mk) - 1 + h
                        dve.wait_ge(sq_ready, N)
                        v.tensor_reduce(var2[h][:], sq[h][:].rearrange("p (b q) -> p b q", q=PROJ), AX.X, ALU.add).then_inc(var2_ready, 1)
                    for h in range(2):
                        N = 2 * upto(ms, mk) - 1 + h
                        uu = u[mk % 2][h]
                        dve.wait_ge(std2_ready, N)
                        v.reciprocal(inv2[h][:], std2[h][:]).then_inc(inv2_ready, 1)
                        b0 = P * ms + HALF * h + UB * mk
                        at = slice(b0, b0 + UB) if isinstance(ms, int) else bass.ds(b0, UB)
                        v.tensor_copy(uu[:, :, PROJ], xt[:, at]).then_inc(u_ready, 1)
                        dve.wait_ge(inv2_ready, N)
                        v.tensor_tensor(uu[:, :, 0:PROJ], b_y[h][:].rearrange("p (b q) -> p b q", q=PROJ),
                                        inv2[h][:].unsqueeze(2).broadcast_to([P, UB, PROJ]), ALU.mult).then_inc(u_ready, 1)
                if prev and k == 2:
                    dve.wait_ge(stdz_ready, s)
                    v.reciprocal(invz[:], stdz[:]).then_inc(invz_ready, 1)
                    dve.wait_ge(invz_ready, s)
                    v.tensor_scalar(zn[:], bf[:, 0:KEEP], invz[:], None, ALU.mult).then_inc(zn_ready, 1)
                if mlp_here(s, k, cur, prev):
                    keep_output(s)
                if cur and not prev:
                    if k == 0:
                        x_rows()
                        sum_coefficients()
                    if k == 1:
                        pair_means()
                    if k == 2:
                        last_pair_rows()

            x_scale()
            projection_weights()
            walk(dve, slot)


def shape_constants():
    rows = [12500, 1000, 12500, 1000, 1000, 1000, 12500, 125000, 1250, 125000, 125000, 1250, 12500, 1250, 12500, 1000,
            1250, 1250, 1250, 12500, 1250, 1250, 1250, 12500, 12500, 1250]
    first = np.concatenate([[0], np.cumsum(rows)[:-1]]).astype(np.int32)
    f = np.arange(CHUNKS * P)
    row_b, row_n = (f // NT).reshape(CHUNKS, P), (f % NT).reshape(CHUNKS, P)
    return first, row_b, row_n


def lay_out(inputs):
    g = {k: np.asarray(v) for k, v in inputs.items()}
    first, row_b, row_n = shape_constants()
    a = {}
    a["table"] = np.concatenate([g[f"tbl_{i}"] for i in range(NT)], axis=0)
    ids = g["ids"].reshape(GROUPS, 2, HALF, NT)
    joined = ids[:, :, row_b, row_n].transpose(3, 0, 2, 1).reshape(P, -1)
    base = np.repeat(first[row_n].T[:, :, None], 2, axis=2).reshape(P, -1)
    a["ids"] = np.ascontiguousarray(np.concatenate([joined, np.zeros_like(base), base], axis=1))
    wsi = g["L0_rec_Wsi"]
    a["wdT"] = np.ascontiguousarray(g["L0_rec_Wd"].T.reshape(DK, P, E).transpose(1, 0, 2))
    a["denT"] = np.ascontiguousarray(g["r_dense_t"].T.reshape(DK, P, BATCH).transpose(1, 0, 2))
    wl, gsi, bsi = g["L0_rec_Wl"], g["L0_rec_gsi"], g["L0_rec_bsi"]
    ti, tj = np.tril_indices(PROJ + 1, k=-1)
    pair = {(int(i), int(j)): n for n, (i, j) in enumerate(zip(ti, tj))}
    wf = np.zeros((4, PROJ, WS, MAXD), np.float32)
    grow, gcol = np.ones((2, 4, PROJ, WS), np.float32)
    moved = np.zeros((4, PROJ, SQ), np.float32)
    M = PROJ // 2
    for c in range(M):
        s, r = c // 4, c % 4
        for p in range(PROJ):
            i, j = (M + c, M + p) if p < c else (p, c)
            moved[r, p, s] = p < c
            grow[r, p, s], gcol[r, p, s] = gsi[i], gsi[j]
            if i > j:
                wf[r, p, s] = wl[:, pair[i + 1, j + 1]]
    for p in range(PROJ):
        wf[0, p, WS - 1] = wl[:, pair[p + 1, 0]]
        grow[0, p, WS - 1] = gsi[p]
    a["wf"] = wf.reshape(P, WS, MAXD)
    wlT = np.zeros((PCH * P, MAXD), np.float32)
    wlT[:NPAIR] = wl.T
    a["wlT"] = np.ascontiguousarray(wlT.reshape(PCH, P, MAXD).transpose(1, 0, 2))
    ce = np.zeros((3, PCH * P, P), np.float32)
    n = np.arange(NPAIR)
    real = tj > 0
    ce[0, n[real], 32 + ti[real] - 1] = 1.0
    ce[1, n[real], 32 + tj[real] - 1] = 1.0
    ce[1, n[~real], 64] = 1.0
    ce[2, n[real], 65] = E
    a["ce"] = np.ascontiguousarray(ce.reshape(3, PCH, P, P).transpose(2, 0, 1, 3)[:, :, :, :SUMS])
    w1 = np.concatenate([g["W_top1"][:KEEP], g["W_top1"][MAXD:]], axis=0)
    w1 = w1.reshape(ZK + DK, P, F1).transpose(1, 0, 2)
    a["w1z"], a["w1d"] = np.ascontiguousarray(w1[:, :ZK]), np.ascontiguousarray(w1[:, ZK:])
    a["w2"] = np.ascontiguousarray(g["W_top2"].reshape(MT1, P, F2).transpose(1, 0, 2))

    cols = np.zeros((P, NCOL), np.float32)

    def put(name, values):
        cols[:, COL[name][0]:COL[name][1]] = values

    put("wsT", np.concatenate([g["L0_rec_Ws"].T] * 2, axis=0))
    put("ident", np.eye(P))
    put("blk", np.kron(np.eye(2), np.ones((D, D))))
    put("gsr", g["L0_rec_gs"])
    put("wrow", wsi.T[row_n].transpose(1, 0, 2).reshape(P, -1))
    own = np.zeros((P, AB), np.float32)
    for unit in PIECES:
        for c, lo, hi, off in unit:
            own[:, off:off + hi - lo + 1] = row_b[c][:, None] == np.arange(lo, hi + 1)
    put("own", own)
    put("gd", g["L0_rec_gd"].reshape(P, 1))
    put("bd", g["L0_rec_bd"].reshape(P, 1))
    put("gl", g["L0_rec_gl"][:KEEP].reshape(ZK, P).T)
    put("bl", g["L0_rec_bl"][:KEEP].reshape(ZK, P).T)
    put("b1", g["b_top1"].reshape(MT1, P).T)
    put("b2", g["b_top2"].reshape(MT2, P).T)
    put("w3", g["W_top3"].reshape(MT2, P).T)
    put("grow", grow.reshape(P, WS))
    put("gcol", gcol.reshape(P, WS))
    put("moved", moved.reshape(P, SQ))

    def pairs(values, x_value):
        full = np.zeros(PCH * P, np.float32)
        full[:NPAIR] = values
        full[:NPAIR][x_value[0]] = x_value[1]
        return full.reshape(PCH, P).T

    never = np.zeros(NPAIR, bool)
    put("gI", pairs(gsi[ti - 1], (never, 0.0)))
    put("hI", pairs(bsi[ti - 1], (never, 0.0)))
    put("gJ", pairs(gsi[np.maximum(tj, 1) - 1], (~real, 1.0)))
    put("hJ", pairs(bsi[np.maximum(tj, 1) - 1], (~real, 0.0)))
    put("eps", EPS)
    cols[65, COL["one_row"][0]] = 1.0
    a["cols"] = cols
    a["brow"] = np.concatenate([g["L0_rec_bs"], wsi.reshape(-1)])[None, :]
    return a


def kernel(**inputs):
    import concourse.bacc as _bacc
    from concourse.bass_utils import run_bass_kernel_spmd as _run

    arrays = lay_out(inputs)
    nc = _bacc.Bacc("TRN2", target_bir_lowering=False, num_devices=1)
    t = {n: nc.dram_tensor("in_" + n, v.shape, mybir.dt.from_np(v.dtype), kind="ExternalInput").ap() for n, v in arrays.items()}
    out = nc.dram_tensor("out", (BATCH, 1), F32, kind="ExternalOutput").ap()
    program(nc, t, out)
    r = _run(nc, [{"in_" + n: v for n, v in arrays.items()}], core_ids=[0])
    return r.results[0]["out"]
```
